# Optimizing a Trainium2 kernel written in Bass

```python
import numpy as np
import jax
import jax.numpy as jnp

def _softmax(x, axis=-1):
    return jax.nn.softmax(x, axis=axis)

def _gelu(x):
    return jax.nn.gelu(x, approximate=True)

def _silu(x):
    return jax.nn.silu(x)

def _sigmoid(x):
    return jax.nn.sigmoid(x)

def _layernorm(x, axis=-1, eps=1e-05):
    m = jnp.mean(x, axis=axis, keepdims=True)
    v = jnp.var(x, axis=axis, keepdims=True)
    return (x - m) / jnp.sqrt(v + eps)

def _scatter_add(tgt, idx, src, axis=0):
    return tgt.at[idx].add(src)

def _segment_sum(src, seg, n):
    return jax.ops.segment_sum(src, seg, n)
kernel_name = 'mk_gnn_ffn_d1_gnn_r8_b87789'

def setup_inputs(seed: int=0):
    np.random.seed(seed)
    _w = jnp.asarray

    def _rec_inputs():
        import jax
        import jax.numpy as jnp
        _gk = jax.random.key(seed)
        x = -8.776e-05 + 1 * jax.random.normal(jax.random.fold_in(_gk, 1), (2500, 256), jnp.float32)
        src = jax.random.randint(jax.random.fold_in(_gk, 2), (40000,), 0, 2500, jnp.int32)
        dst = jax.random.randint(jax.random.fold_in(_gk, 3), (40000,), 0, 2500, jnp.int32)
        _o = jnp.argsort(dst, stable=True)
        src = src[_o]
        dst = dst[_o]
        edge_type_8 = jax.random.randint(jax.random.fold_in(_gk, 12), (40000,), 0, 8, jnp.int32)
        return (x, src, dst, edge_type_8)
    x, src, dst, edge_type_8 = _rec_inputs()

    def _L0_gnn_setup():
        import jax, jax.numpy as jnp
        import numpy as np
        N_NODES = 2500
        N_EDGES = 40000
        D = 256
        R = 8

        def _xavier(key, shape):
            fan_in, fan_out = (shape[-2], shape[-1])
            bound = float(np.sqrt(6.0 / (fan_in + fan_out)))
            return jax.random.uniform(key, shape, jnp.float32, -bound, bound)

        def _rgcn_layer(x, W, self_w, b, src, dst, edge_type, num_nodes):
            xW = jnp.einsum('ni,rio->rno', x, W)
            msg = xW[edge_type, src]
            agg = jax.ops.segment_sum(msg, dst, num_segments=num_nodes)
            return agg + x @ self_w + b
        key = jax.random.key(seed)
        ks = jax.random.split(key, 10)
        x = jax.random.normal(ks[0], (N_NODES, D), jnp.float32)
        edge_index = jax.random.randint(ks[1], (2, N_EDGES), 0, N_NODES)
        edge_type = jax.random.randint(ks[2], (N_EDGES,), 0, R)
        W1 = _xavier(ks[3], (R, D, D))
        self_w1 = _xavier(ks[4], (D, D))
        b1 = jnp.zeros((D,), jnp.float32)
        W2 = _xavier(ks[5], (R, D, D))
        self_w2 = _xavier(ks[6], (D, D))
        b2 = jnp.zeros((D,), jnp.float32)
        return {'x': x, 'W1': W1, 'self_w1': self_w1, 'b1': b1, 'W2': W2, 'self_w2': self_w2, 'b2': b2, 'edge_index': edge_index, 'edge_type': edge_type}
    _L0_gnn_all = _L0_gnn_setup()
    _L0_gnn_in = {k: v for k, v in _L0_gnn_all.items() if k in ('W1', 'self_w1', 'b1', 'W2', 'self_w2', 'b2')}
    del _L0_gnn_all

    def _L0_ffn_setup():
        import math
        import jax, jax.numpy as jnp
        import numpy as np
        CAPACITY_FACTOR = 1.25
        key = jax.random.key(seed)
        ks = jax.random.split(key, 5)
        B, L, D, F, E = (8, 1024, 256, 1024, 8)
        h = jax.random.normal(ks[0], (B, L, D), dtype=jnp.float32)
        gate_w = jax.random.normal(ks[1], (D, E), dtype=jnp.float32) * 0.02
        gate_b = jnp.zeros((E,), dtype=jnp.float32)
        w1 = jax.random.normal(ks[2], (E, D, F), dtype=jnp.float32) * (1.0 / math.sqrt(D))
        b1 = jnp.zeros((E, F), dtype=jnp.float32)
        w2 = jax.random.normal(ks[3], (E, F, D), dtype=jnp.float32) * (1.0 / math.sqrt(F))
        b2 = jnp.zeros((E, D), dtype=jnp.float32)
        return {'h': h, 'gate_w': gate_w, 'gate_b': gate_b, 'w1': w1, 'b1': b1, 'w2': w2, 'b2': b2}
    _L0_ffn_all = _L0_ffn_setup()
    _L0_ffn_in = {k: v for k, v in _L0_ffn_all.items() if k in ('gate_w', 'gate_b', 'w1', 'b1', 'w2', 'b2')}
    del _L0_ffn_all
    return {'x': x, 'src': src, 'dst': dst, 'edge_type_8': edge_type_8, 'L0_gnn_W1': _L0_gnn_in['W1'], 'L0_gnn_self_w1': _L0_gnn_in['self_w1'], 'L0_gnn_b1': _L0_gnn_in['b1'], 'L0_gnn_W2': _L0_gnn_in['W2'], 'L0_gnn_self_w2': _L0_gnn_in['self_w2'], 'L0_gnn_b2': _L0_gnn_in['b2'], 'L0_ffn_gate_w': _L0_ffn_in['gate_w'], 'L0_ffn_gate_b': _L0_ffn_in['gate_b'], 'L0_ffn_w1': _L0_ffn_in['w1'], 'L0_ffn_b1': _L0_ffn_in['b1'], 'L0_ffn_w2': _L0_ffn_in['w2'], 'L0_ffn_b2': _L0_ffn_in['b2']}

def reference(x, src, dst, edge_type_8, L0_gnn_W1, L0_gnn_self_w1, L0_gnn_b1, L0_gnn_W2, L0_gnn_self_w2, L0_gnn_b2, L0_ffn_gate_w, L0_ffn_gate_b, L0_ffn_w1, L0_ffn_b1, L0_ffn_w2, L0_ffn_b2):
    import jax
    import jax.numpy as jnp

    def _L0_gnn_ref(x, W1, self_w1, b1, W2, self_w2, b2, edge_index, edge_type):
        import jax, jax.numpy as jnp
        import numpy as np
        N_NODES = 2500
        N_EDGES = 40000
        D = 256
        R = 8

        def _xavier(key, shape):
            fan_in, fan_out = (shape[-2], shape[-1])
            bound = float(np.sqrt(6.0 / (fan_in + fan_out)))
            return jax.random.uniform(key, shape, jnp.float32, -bound, bound)

        def _rgcn_layer(x, W, self_w, b, src, dst, edge_type, num_nodes):
            xW = jnp.einsum('ni,rio->rno', x, W)
            msg = xW[edge_type, src]
            agg = jax.ops.segment_sum(msg, dst, num_segments=num_nodes)
            return agg + x @ self_w + b
        src, dst = (edge_index[0], edge_index[1])
        h = _rgcn_layer(x, W1, self_w1, b1, src, dst, edge_type, N_NODES)
        h = jax.nn.relu(h)
        out = _rgcn_layer(h, W2, self_w2, b2, src, dst, edge_type, N_NODES)
        return out

    def _L0_ffn_ref(h, gate_w, gate_b, w1, b1, w2, b2):
        import math
        import jax, jax.numpy as jnp
        import numpy as np
        CAPACITY_FACTOR = 1.25
        B, L, D = h.shape
        E = gate_w.shape[1]
        T = B * L
        C = max(1, math.ceil(CAPACITY_FACTOR * T / E))
        x = h.reshape(T, D)
        logits = x @ gate_w + gate_b
        probs = jax.nn.softmax(logits, axis=-1)
        idx = jnp.argmax(probs, axis=-1)
        prb = jnp.take_along_axis(probs, idx[:, None], axis=1)[:, 0]
        one_hot = jax.nn.one_hot(idx, E, dtype=jnp.float32)
        pos = (jnp.cumsum(one_hot, axis=0) * one_hot).sum(-1).astype(jnp.int32) - 1
        kept = pos < C
        pos_safe = jnp.where(kept, pos, C)
        buf = jnp.zeros((E, C, D), dtype=h.dtype).at[idx, pos_safe].set(x, mode='drop')
        hmid = jax.nn.relu(jnp.einsum('ecd,edf->ecf', buf, w1) + b1[:, None, :])
        ybuf = jnp.einsum('ecf,efd->ecd', hmid, w2) + b2[:, None, :]
        pos_g = jnp.minimum(pos, C - 1)
        y_tok = ybuf[idx, pos_g] * (prb * kept)[:, None]
        y = y_tok.reshape(B, L, D)
        y = jnp.nan_to_num(y, nan=0.0, posinf=10000.0, neginf=-10000.0)
        return y
    edge_index = jnp.stack([src, dst])
    x = x + _L0_gnn_ref(_layernorm(x, axis=-1), L0_gnn_W1, L0_gnn_self_w1, L0_gnn_b1, L0_gnn_W2, L0_gnn_self_w2, L0_gnn_b2, edge_index, edge_type_8)
    x = x + _L0_ffn_ref(_layernorm(x, axis=-1)[None], L0_ffn_gate_w, L0_ffn_gate_b, L0_ffn_w1, L0_ffn_b1, L0_ffn_w2, L0_ffn_b2)[0]
    return x

_drawn_inputs = setup_inputs


def setup_inputs(seed=0):
    import zlib

    import numpy as np

    out = dict(_drawn_inputs(seed))
    spreads = {'L0_gnn_b1': (0.0, 0.288),
     'L0_gnn_b2': (0.0, 0.8),
     'L0_ffn_gate_b': (0.0, 0.8),
     'L0_ffn_b1': (0.0, 0.8),
     'L0_ffn_b2': (0.0, 2.0)}
    factors = {'L0_ffn_gate_w': 8.0, 'L0_ffn_w1': 8.0, 'L0_ffn_w2': 7.805}
    for name, (base, spread) in spreads.items():
        noise = np.random.default_rng([zlib.crc32(name.encode()), seed]).standard_normal(out[name].shape)
        drawn = base * np.exp(spread * noise) if base else spread * noise
        out[name] = jnp.asarray(drawn.astype(out[name].dtype))
    for name, factor in factors.items():
        out[name] = (out[name] * factor).astype(out[name].dtype)
    return out
```

```python
from contextlib import ExitStack

import numpy as np
import concourse.bass as bass
from concourse import mybir

F32 = mybir.dt.float32
I32 = mybir.dt.int32
U32 = mybir.dt.uint32
ALU = mybir.AluOpType
ACT = mybir.ActivationFunctionType
AX = mybir.AxisListType

N, D, R, E = 2500, 256, 8, 40000
P = 125
NK = N // P
H = D // 128
TERMS = R + 1
CHUNKS = E // P
GROUP_CHUNKS = 32
GROUPS = CHUNKS // GROUP_CHUNKS
WIN = 16
KEYS = R * WIN
GROUP_WIN = 288
WINDOW_PASSES = -(-N // WIN)
NPAD = ((WINDOW_PASSES - 1) * WIN + GROUP_WIN + 127) // 128 * 128
EDGE_TILE, EDGE_TILES = 80, 4
RING = 16
HOTS = 4
STAGE = 8
STAGES = GROUP_CHUNKS // STAGE
SPAN = GROUP_WIN * R * H
SUMMED_CREDIT = RING + STAGE + 1
W_STEPS = R * H * H
SELF_BLOCKS = 5
SELF_COLS = N // SELF_BLOCKS
EPS = 1e-5

EXPERTS, FF = 8, 1024
FT = FF // 128
CAP = -(-5 * N // (4 * EXPERTS))
SLOT_TILE, SLOT_TILES = 98, 4
SLOTS = SLOT_TILE * SLOT_TILES
assert CAP <= SLOTS and GROUPS % 2 == 0 and RING % STAGE == 0 and GROUP_CHUNKS % RING == 0
FLT_MAX = 3.4028234663852886e38
NAN_INF_TO = 10000.0


def w_steps_after(u):
    first, slots = 2, GROUP_CHUNKS - 4
    done = lambda v: min(W_STEPS, max(0, (v - first) * W_STEPS // slots))
    return range(done(u), done(u + 1))


def build(nc, io, out):
    with ExitStack() as ctx:
        def sb(name, shape, dt=F32):
            return ctx.enter_context(nc.sbuf_tensor(name, shape, dt))

        def sem(name):
            return ctx.enter_context(nc.semaphore(name))

        table = [nc.dram_tensor(f"table{l}", (N, D), F32, kind="Internal").ap() for l in range(2)]
        disp = nc.dram_tensor("dispatched", (EXPERTS * SLOTS, D), F32, kind="Internal").ap()
        ybuf = nc.dram_tensor("expert_out", (EXPERTS * SLOTS, 2 * D), F32, kind="Internal").ap()

        x_rows = sb("x_rows", [P, NK, D])
        f_rows = sb("f_rows", [P, NK, D])
        cols = [sb(f"cols{i}", [128, H, NPAD]) for i in range(2)]
        accum = sb("accum", [128, 2 * SPAN])
        weights = [sb(f"weights{l}", [128, H, TERMS, D]) for l in range(2)]
        ring = sb("ring", [P, RING, D])
        hot = sb("hot", [P, HOTS, KEYS])
        ring_flat = ring[:, :, :].rearrange("p q d -> p (q d)")
        edges_i = ring_flat[:EDGE_TILE, 0:1500].bitcast(I32).rearrange("q (j t e) -> q j t e", j=3, t=EDGE_TILES)
        edges_f = ring_flat[:EDGE_TILE, 1500:3000].rearrange("q (j t e) -> q j t e", j=3, t=EDGE_TILES)
        edges_t = sb("edges_t", [P, 3, CHUNKS])
        spans = sb("spans", [EDGE_TILE, 2, EDGE_TILES])
        low, spread, place_in_group = (ring_flat[0:1, 3000 + i * CHUNKS:3000 + (i + 1) * CHUNKS] for i in range(3))
        first_start = sb("first_start", [1, CHUNKS])[:, :]
        flag = sb("flag", [1, 16])
        start_row = sb("start_row", [1, CHUNKS])
        off_f = sb("off_f", [1, CHUNKS])
        off_i = sb("off_i", [1, CHUNKS], I32)
        base_i = sb("base_i", [1, GROUPS], I32)
        passes_i = sb("passes_i", [1, 1], I32)
        key = sb("key", [P, CHUNKS])
        key_t = sb("key_t", [P, 3, CHUNKS])
        stage = sb("stage", [P, STAGES, STAGE], U32)
        ident = sb("ident", [128, 128])
        tri = sb("tri", [P, P])
        ones = sb("ones", [1, 128])
        zeros = sb("zeros", [128, 4 * D])
        key_iota_i = sb("key_iota_i", [P, KEYS], I32)
        key_iota = sb("key_iota", [P, KEYS])
        e_iota_i = sb("e_iota_i", [P, EXPERTS], I32)
        e_iota = sb("e_iota", [P, EXPERTS])
        bias_rows = sb("bias_rows", [EXPERTS * FT + 2 * H, 128])
        bias_cols = sb("bias_cols", [128, EXPERTS * FT + 2 * H])
        stats = sb("stats", [P, NK, 6])
        ln = sb("ln", [P, 8, NK])
        gate_w = sb("gate_w", [128, H, EXPERTS])
        gate_b = sb("gate_b", [P, EXPERTS])
        lg = sb("lg", [P, 4, NK, EXPERTS])
        picked = sb("picked", [P, EXPERTS, NK])
        counts = sb("counts", [P, EXPERTS, NK])
        tok = sb("tok", [P, 12, NK])
        slot_to = sb("slot_to", [P, NK], U32)
        slot_from = sb("slot_from", [P, NK], U32)
        y_finite = sb("y_finite", [SLOT_TILE, 2, D], mybir.dt.uint8)

        ew1 = [accum[:, i * 4096:i * 4096 + 2048].rearrange("p (h f) -> p h f", h=H) for i in range(2)]
        ew2 = [accum[:, i * 4096 + 2048:(i + 1) * 4096].rearrange("p (t d) -> p t d", t=FT) for i in range(2)]
        hmid = [cols[i][:, :, :].rearrange("p h n -> p (h n)")[:, 0:FT * SLOTS].rearrange("p (t n) -> p t n", t=FT)
                for i in range(2)]
        wflat = [weights[i][:, :, :, :].rearrange("p h t d -> p (h t d)") for i in range(2)]
        slot_rows = [wflat[i][:SLOT_TILE, 0:1024].rearrange("p (j d) -> p j d", j=SLOT_TILES) for i in range(2)]
        y_rows = [wflat[i][:SLOT_TILE, 1024:3072].rearrange("p (j s d) -> p j s d", j=SLOT_TILES, s=2) for i in range(2)]
        slot_cols = [wflat[i][:, 3072:3072 + H * SLOTS].rearrange("p (h n) -> p h n", h=H) for i in range(2)]
        y_tok = [accum[:P, k * 2 * D:(k + 1) * 2 * D] for k in range(2 * SPAN // (2 * D))]
        y_tok += [ring[:, 2 * j:2 * j + 2, :].rearrange("p a d -> p (a d)") for j in range(NK - len(y_tok))]
        y_raw = [f_rows[:SLOT_TILE, i, :] for i in range(2)]
        y_over = [f_rows[:SLOT_TILE, 2 + i, :] for i in range(2)]
        b2 = f_rows[:SLOT_TILE, NK - EXPERTS:NK, :]
        y_under = [f_rows[:SLOT_TILE, 4 + i, :] for i in range(2)]

        bank = [ctx.enter_context(nc.psum_tensor(f"bank{i}", [128, 512], F32)) for i in range(8)]
        chunk_sum = [bank[4 + i][:, 0:H * KEYS].rearrange("p (h k) -> p h k", h=H) for i in range(HOTS)]

        edges_in, gate_in, bias_in, b2_in = sem("edges_in"), sem("gate_in"), sem("bias_in"), sem("b2_in")
        x_in = [sem(f"x_in{i}") for i in range(4)]
        weights_in = [sem("weights_in0"), sem("weights_in1")]
        consts = sem("consts")
        dve_consts = sem("dve_consts")
        edges_as_f, spans_done = sem("edges_as_f"), sem("spans_done")
        edges_turned, spans_turned = sem("edges_turned"), sem("spans_turned")
        edges_copied = sem("edges_copied")
        bias_turned, bias_copied = sem("bias_turned"), sem("bias_copied")
        var_ready, std_ready = sem("var_ready"), sem("std_ready")
        rows_ready = sem("rows_ready")
        turned, turned_used = sem("turned"), sem("turned_used")
        passes_ready = sem("passes_ready")
        disp_zero, disp_in = sem("disp_zero"), sem("disp_in")
        L = []
        for l in range(2):
            s = lambda name: sem(f"{name}_{l}")
            L.append(dict(
                table_in=s("table_in"), rows_out=s("rows_out"), starts=s("starts"), starts_wide=s("starts_wide"),
                keyed=s("keyed"), staged=s("staged"), slot=[s(f"slot{q}") for q in range(RING)],
                hot=s("hot"), summed=s("summed"), added=s("added"), zeroed=s("zeroed"), w_done=s("w_done"),
                w_added=s("w_added"), self_done=s("self_done"), self_out=s("self_out"), cols_in=s("cols_in"),
                complete=s("complete"), relu=s("relu"), back=s("back"), back_a=s("back_a"), back_v=s("back_v"),
                claimed=s("claimed")))
        logits_done, scores_ready, exps_ready = sem("logits_done"), sem("scores_ready"), sem("exps_ready")
        totals_ready, before_ready = sem("totals_ready"), sem("before_ready")
        slots_ready = sem("slots_ready")
        ew_in = [sem("ew_in0"), sem("ew_in1")]
        slot_rows_in = [sem("slot_rows_in0"), sem("slot_rows_in1")]
        slots_turned, slot_cols_v, slot_cols_a = sem("slots_turned"), sem("slot_cols_v"), sem("slot_cols_a")
        mid_done, mid_a, mid_v = sem("mid_done"), sem("mid_a"), sem("mid_v")
        y_done, y_taken, y_ready = sem("y_done"), sem("y_taken"), sem("y_ready")
        y_stored = [sem("y_stored0"), sem("y_stored1")]
        y_in = [sem(f"y_in{i}") for i in range(NK)]
        out_ready, out_stored = sem("out_ready"), sem("out_stored")

        def passes_of(eng):
            eng.wait_ge(passes_ready, 1)
            return eng.value_load(passes_i[0:1, 0:1], min_val=1, max_val=WINDOW_PASSES)

        def strided_cols(buf, h, k0, nk):
            return buf[:, h, 0:N].rearrange("c (p k) -> c k p", k=NK)[:, k0:k0 + nk, :]

        block = ctx.enter_context(nc.Block())

        @block.sync
        def _(sp):
            x_v = io["x"].rearrange("(p k) d -> p k d", k=NK)
            for j, name in enumerate(("dst", "edge_type_8", "src")):
                sp.dma_start(edges_i[:, j, :, :],
                             io[name].rearrange("(t q e) -> q t e", q=EDGE_TILE, e=P)).then_inc(edges_in, 16)
            for i in range(4):
                sp.dma_start(x_rows[:, 5 * i:5 * i + 5, :], x_v[:, 5 * i:5 * i + 5, :]).then_inc(x_in[i], 16)
            sp.dma_start(bias_rows[0:EXPERTS * FT, :], io["L0_ffn_b1"].rearrange("e (t c) -> (e t) c", c=128))\
              .then_inc(bias_in, 16)
            for l in range(2):
                at = EXPERTS * FT + H * l
                sp.dma_start(bias_rows[at:at + H, :], io[f"L0_gnn_b{l + 1}"].rearrange("(h c) -> h c", c=128))\
                  .then_inc(bias_in, 16)

            def load_weights(l):
                for h in range(H):
                    sp.dma_start(weights[l][:, h, 0:R, :],
                                 io[f"L0_gnn_W{l + 1}"][:, h * 128:h * 128 + 128, :].rearrange("r c o -> c r o"))\
                      .then_inc(weights_in[l], 16)
                    sp.dma_start(weights[l][:, h, R, :], io[f"L0_gnn_self_w{l + 1}"][h * 128:h * 128 + 128, :])\
                      .then_inc(weights_in[l], 16)

            t_v = table[0].rearrange("(p k) d -> p k d", k=NK)
            for i in range(5):
                sp.wait_ge(rows_ready, 4 * i + 4)
                sp.dma_start(t_v[:, 4 * i:4 * i + 4, :], f_rows[:, 4 * i:4 * i + 4, :]).then_inc(L[0]["table_in"], 16)
            load_weights(0)
            sp.wait_ge(consts, 1)
            for e in range(EXPERTS):
                sp.dma_start(disp[e * SLOTS:(e + 1) * SLOTS, :].rearrange("(p j) d -> p (j d)", j=SLOT_TILES),
                             zeros[0:SLOT_TILE, :]).then_inc(disp_zero, 16)
            load_weights(1)
            sp.dma_start(gate_w[:, :, :], io["L0_ffn_gate_w"].rearrange("(h c) e -> c h e", c=128)).then_inc(gate_in, 16)
            sp.dma_start(gate_b[:, :], io["L0_ffn_gate_b"].rearrange("(a e) -> a e", a=1).to_broadcast([P, EXPERTS]))\
              .then_inc(gate_in, 16)
            t_v = table[1].rearrange("(p k) d -> p k d", k=NK)
            for i in range(5):
                sp.wait_ge(L[0]["back_a"], i + 1)
                sp.wait_ge(L[0]["back_v"], i + 1)
                sp.dma_start(t_v[:, 4 * i:4 * i + 4, :], f_rows[:, 4 * i:4 * i + 4, :]).then_inc(L[1]["table_in"], 16)

            def load_expert(e, v):
                sp.dma_start(ew1[v], io["L0_ffn_w1"][bass.ds(e, 1), :, :].rearrange("a (h c) f -> c (a h) f", c=128))\
                  .then_inc(ew_in[v], 16)
                sp.dma_start(ew2[v], io["L0_ffn_w2"][bass.ds(e, 1), :, :].rearrange("a (t c) d -> c (a t) d", c=128))\
                  .then_inc(ew_in[v], 16)

            sp.wait_ge(L[1]["complete"], 1)
            load_expert(0, 0)
            load_expert(1, 1)
            sp.wait_ge(disp_in, NK * 16)
            sp.dma_start(b2.rearrange("p e d -> p (e d)"),
                         io["L0_ffn_b2"].rearrange("(a e) d -> a (e d)", a=1).to_broadcast([SLOT_TILE, EXPERTS * D]))\
              .then_inc(b2_in, 16)
            with sp.Fori(1, EXPERTS // 2) as pair:
                for v in range(2):
                    sp.wait_ge(y_done, (pair * 2 + (v - 1)) * SLOT_TILES)
                    load_expert(pair * 2 + v, v)
            out_v = out.rearrange("(p k) d -> p k d", k=NK)
            for i in range(5):
                sp.wait_ge(out_ready, 4 * i + 4)
                sp.dma_start(out_v[:, 4 * i:4 * i + 4, :], x_rows[:, 4 * i:4 * i + 4, :]).then_inc(out_stored, 16)
            sp.wait_ge(out_stored, 5 * 16)

        @block.gpsimd
        def _(pool):
            pool.memset(zeros[:, :], 0.0).then_inc(consts, 1)
            pool.memset(ident[:, :], 0.0)
            pool.memset(tri[:, :], 1.0)
            pool.memset(ones[:, :], 1.0)
            pool.iota(key_iota_i[:, :], pattern=[[1, KEYS]], base=0, channel_multiplier=0)
            pool.iota(e_iota_i[:, :], pattern=[[1, EXPERTS]], base=0, channel_multiplier=0)
            pool.drain()
            pool.affine_select(out=ident[:, :], in_=ident[:, :], compare_op=ALU.not_equal, fill=1.0, base=0,
                               pattern=[[-1, 128]], channel_multiplier=1)
            pool.affine_select(out=tri[:, :], in_=tri[:, :], compare_op=ALU.is_gt, fill=0.0, base=0,
                               pattern=[[1, P]], channel_multiplier=-1)
            pool.tensor_copy(key_iota[:, :], key_iota_i[:, :])
            pool.tensor_copy(e_iota[:, :], e_iota_i[:, :])
            pool.drain().then_inc(consts, 1)

            for l in range(2):
                S = L[l]
                passes = passes_of(pool)
                with pool.Fori(0, passes) as k:
                    with pool.Fori(0, GROUPS) as g:
                        for u in range(GROUP_CHUNKS):
                            q = u % RING
                            if u % STAGE == 0:
                                pool.wait_ge(S["staged"], k * (GROUPS * STAGES) + g * STAGES + (u // STAGE + 1))
                            pool.wait_ge(S["summed"], k * CHUNKS + g * GROUP_CHUNKS + (u + SUMMED_CREDIT - RING + 1))
                            pool.sem_inc(S["claimed"], 1)
                            pool.wait_ge(S["table_in"], 5 * 16)
                            pool.indirect_dma_start(
                                ring[:, q, :], None, table[l],
                                bass.IndirectOffsetOnAxis(ap=stage[:, u // STAGE, u % STAGE:u % STAGE + 1], axis=0),
                            ).then_inc(S["slot"][q], 16)

            pool.wait_ge(disp_zero, EXPERTS * 16)
            pool.wait_ge(slots_ready, 1)
            for k in range(NK):
                pool.indirect_dma_start(
                    disp, bass.IndirectOffsetOnAxis(ap=slot_to[:, k:k + 1], axis=0), f_rows[:, k, :], None,
                    bounds_check=EXPERTS * SLOTS - 1, oob_is_err=False).then_inc(disp_in, 16)
            pool.wait_ge(disp_in, NK * 16)

            def load_slots(e, v):
                pool.dma_start(slot_rows[v], disp[bass.ds(e * SLOTS, SLOTS), :]
                               .rearrange("(p j) d -> p j d", j=SLOT_TILES)).then_inc(slot_rows_in[v], 16)

            def store_y(e, v):
                pool.wait_ge(y_ready, e * SLOT_TILES + SLOT_TILES)
                pool.dma_start(ybuf[bass.ds(e * SLOTS, SLOTS), :].rearrange("(p j) d -> p j d", j=SLOT_TILES),
                               y_rows[v].rearrange("p j s d -> p j (s d)")).then_inc(y_stored[v], 16)

            load_slots(0, 0)
            load_slots(1, 1)
            with pool.Fori(0, EXPERTS // 2 - 1) as pair:
                for v in range(2):
                    pool.wait_ge(slots_turned, pair * (2 * H) + (v + 1) * H)
                    load_slots(pair * 2 + (v + 2), v)
                    store_y(pair * 2 + v, v)
            for v in range(2):
                store_y(EXPERTS - 2 + v, v)
            for v in range(2):
                pool.wait_ge(y_stored[v], EXPERTS // 2 * 16)
            for k in range(NK):
                pool.indirect_dma_start(
                    y_tok[k], None, ybuf, bass.IndirectOffsetOnAxis(ap=slot_from[:, k:k + 1], axis=0),
                ).then_inc(y_in[k], 16)

        @block.scalar
        def _(act):
            act.wait_ge(edges_in, 3 * 16)
            for j in range(3):
                nc.scalar.activation(edges_f[:, j], edges_i[:, j], ACT.Copy).then_inc(edges_as_f, 1)
            act.wait_ge(edges_turned, 3)
            nc.scalar.activation(edges_t[:, 0, :], bank[4][:P, 0:CHUNKS], ACT.Copy).then_inc(edges_copied, 1)
            nc.scalar.activation(edges_t[:, 1, :], bank[5][:P, 0:CHUNKS], ACT.Copy, scale=float(WIN), bias=1.0)\
                .then_inc(edges_copied, 1)
            nc.scalar.activation(edges_t[:, 2, :], bank[6][:P, 0:CHUNKS], ACT.Copy).then_inc(edges_copied, 1)
            act.wait_ge(bias_turned, 1)
            nc.scalar.activation(bias_cols[:, :], bank[3][:, 0:EXPERTS * FT + 2 * H], ACT.Copy)\
                .then_inc(bias_copied, 1)
            act.wait_ge(var_ready, 1)
            nc.scalar.activation(ln[:, 3, :], ln[:, 2, :], ACT.Sqrt).then_inc(std_ready, 1)

            def turned_out(first, count, per, dest):
                for i in range(count):
                    act.wait_ge(turned, first + i + 1)
                    nc.scalar.activation(dest(i), bank[4 + (first + i) % 4][:, 0:4 * per]
                                         .rearrange("c (k p) -> c k p", k=4), ACT.Copy).then_inc(turned_used, 1)

            def dest_cols(buf):
                return lambda i: strided_cols(buf, i % H, 4 * (i // H), 4)

            turned_out(0, 5 * H, P, dest_cols(cols[0]))

            for l in range(2):
                S = L[l]
                act.wait_ge(bias_copied, 1)
                at = EXPERTS * FT + H * l
                for i in range(SELF_BLOCKS * H):
                    b, h = i // H, i % H
                    act.wait_ge(S["self_done"], i + 1)
                    nc.scalar.activation(cols[1 - l][:, h, b * SELF_COLS:(b + 1) * SELF_COLS],
                                         bank[4 + i % 4][:, 0:SELF_COLS], ACT.Identity,
                                         bias=bias_cols[:, at + h:at + h + 1]).then_inc(S["self_out"], 1)

                def stage_indices(k, g, s):
                    act.wait_ge(S["summed"], k * CHUNKS + g * GROUP_CHUNKS + (STAGE * s + 1))
                    nc.scalar.activation(stage[:, s, :], edges_t[:, 2, bass.ds(g * GROUP_CHUNKS + s * STAGE, STAGE)],
                                         ACT.Copy).then_inc(S["staged"], 1)

                passes = passes_of(act)
                with act.Fori(0, passes) as k:
                    with act.Fori(0, GROUPS) as g:
                        for s in range(STAGES - 1):
                            stage_indices(k, g, s)
                        act.wait_ge(S["w_done"], k * (GROUPS * H) + g * H + 2)
                        nc.scalar.activation(
                            accum[:, bass.ds((g % 2) * SPAN, SPAN)].rearrange("c (a b) -> c a b", b=GROUP_WIN),
                            zeros[:, None, 0:GROUP_WIN].to_broadcast([128, R * H, GROUP_WIN]), ACT.Copy)\
                            .then_inc(S["zeroed"], 1)
                        stage_indices(k, g, STAGES - 1)
                if l == 0:
                    act.wait_ge(S["complete"], 1)
                    nc.scalar.activation(cols[1][:, 1, 0:N], cols[1][:, 1, 0:N], ACT.Relu).then_inc(S["relu"], 1)
                    for i in range(0, NK // 2, 2):
                        act.wait_ge(S["back"], i + 1)
                        nc.scalar.activation(f_rows[:, 2 * i:2 * i + 2, :],
                                             bank[4 + i % 4][:P, :].rearrange("p (k d) -> p k d", k=2), ACT.Copy)\
                            .then_inc(S["back_a"], 1)

            act.wait_ge(var_ready, 2)
            nc.scalar.activation(ln[:, 3, :], ln[:, 2, :], ACT.Sqrt).then_inc(std_ready, 1)
            turned_out(5 * H, 5 * H, P, dest_cols(cols[1]))
            act.wait_ge(scores_ready, 1)
            nc.scalar.activation(lg[:, 1], lg[:, 0], ACT.Exp).then_inc(exps_ready, 1)

            def expert(e, v):
                act.wait_ge(slots_turned, e * H + 2)
                nc.scalar.activation(slot_cols[v][:, 1, :], bank[5][:, 0:SLOTS], ACT.Copy).then_inc(slot_cols_a, 1)
                for t in range(0, FT, 2):
                    act.wait_ge(mid_done, e * FT + (t + 1))
                    nc.scalar.activation(hmid[v][:, t, :], bank[t % 4][:, 0:SLOTS], ACT.Relu,
                                         bias=bias_cols[:, bass.ds(e * FT + t, 1)]).then_inc(mid_a, 1)

            with act.Fori(0, EXPERTS // 2) as pair:
                for v in range(2):
                    expert(pair * 2 + v, v)

        @block.tensor
        def _(pe):
            pe.wait_ge(consts, 2)
            for j in range(3):
                pe.wait_ge(edges_as_f, j + 1)
                for t in range(EDGE_TILES):
                    last = nc.tensor.transpose(bank[4 + j][:P, t * EDGE_TILE:(t + 1) * EDGE_TILE], edges_f[:, j, t, :],
                                               ident[0:EDGE_TILE, 0:EDGE_TILE])
                last.then_inc(edges_turned, 1)
            pe.wait_ge(spans_done, 1)
            for m in range(2):
                for t in range(EDGE_TILES):
                    last = nc.tensor.matmul(bank[m][0:1, t * EDGE_TILE:(t + 1) * EDGE_TILE], spans[:, m, t:t + 1],
                                            ident[0:EDGE_TILE, 0:EDGE_TILE], start=True, stop=True)
            last.then_inc(spans_turned, 1)
            pe.wait_ge(bias_in, 3 * 16)
            nb = EXPERTS * FT + 2 * H
            nc.tensor.transpose(bank[3][:, 0:nb], bias_rows[:, :], ident[0:nb, 0:nb]).then_inc(bias_turned, 1)

            def turn_rows(first, rows, ready):
                for i in range(5 * H):
                    k0, h, n = 4 * (i // H), i % H, first + i
                    pe.wait_ge(rows_ready, ready + k0 + 4)
                    if i >= 4:
                        pe.wait_ge(turned_used, n - 3)
                    for j in range(4):
                        last = nc.tensor.transpose(bank[4 + n % 4][:, j * P:(j + 1) * P],
                                                   rows[:, k0 + j, h * 128:(h + 1) * 128], ident[0:P, 0:P])
                    last.then_inc(turned, 1)

            pe.wait_ge(edges_copied, 3)
            turn_rows(0, f_rows, 0)

            for l in range(2):
                S = L[l]
                pe.sem_inc(S["summed"], SUMMED_CREDIT)
                pe.sem_inc(S["w_done"], 2 * H)
                feats = cols[l]
                if l == 0:
                    pe.wait_ge(turned_used, 5 * H)
                else:
                    pe.wait_ge(L[0]["relu"], 2)
                    pe.wait_ge(L[0]["back_a"], 5)
                    pe.wait_ge(L[0]["back_v"], 5)
                pe.wait_ge(weights_in[l], 2 * H * 16)
                for i in range(SELF_BLOCKS * H):
                    b, ho = i // H, i % H
                    if i >= 4:
                        pe.wait_ge(S["self_out"], i - 3)
                    for h in range(H):
                        last = nc.tensor.matmul(bank[4 + i % 4][:, 0:SELF_COLS],
                                                weights[l][:, h, R, ho * 128:(ho + 1) * 128],
                                                feats[:, h, b * SELF_COLS:(b + 1) * SELF_COLS],
                                                start=(h == 0), stop=(h == H - 1))
                    last.then_inc(S["self_done"], 1)
                pe.wait_ge(S["self_out"], SELF_BLOCKS * H)

                def weight_step(k, g, w):
                    ho, r, h = w // (R * H), w % (R * H) // H, w % H
                    if w == 0:
                        pe.wait_ge(S["added"], k * CHUNKS + g * GROUP_CHUNKS + HOTS)
                    if r == h == 0:
                        pe.wait_ge(S["w_added"], k * (GROUPS * H) + (g - 1) * H + (ho + 1))
                    at = ((g - 1) % 2) * SPAN + (h * R + r) * GROUP_WIN
                    ins = nc.tensor.matmul(bank[2 + ho][:, 0:GROUP_WIN], weights[l][:, h, r, ho * 128:(ho + 1) * 128],
                                           accum[:, bass.ds(at, GROUP_WIN)],
                                           start=(r == h == 0), stop=(w % (R * H) == R * H - 1))
                    if w % (R * H) == R * H - 1:
                        ins.then_inc(S["w_done"], 1)

                def group(k, g, first=False):
                    for u in range(GROUP_CHUNKS):
                        q = u % RING
                        pe.wait_ge(S["slot"][q], k * (CHUNKS // RING * 16) + g * (GROUP_CHUNKS // RING * 16)
                                   + (u // RING + 1) * 16)
                        pe.wait_ge(S["hot"], k * CHUNKS + g * GROUP_CHUNKS + (u + 1))
                        pe.wait_ge(S["added"], k * CHUNKS + g * GROUP_CHUNKS + (u + 1))
                        for h in range(H):
                            last = nc.tensor.matmul(chunk_sum[u % HOTS][:, h, :], ring[:, q, h * 128:(h + 1) * 128],
                                                    hot[:, u % HOTS, :], start=True, stop=True)
                        last.then_inc(S["summed"], 1)
                        if not first:
                            for w in w_steps_after(u):
                                weight_step(k, g, w)

                passes = passes_of(pe)
                with pe.Fori(0, passes) as k:
                    pe.wait_ge(S["starts"], k + 1)
                    nc.tensor.matmul(bank[0][:P, 0:CHUNKS], ones[0:1, 0:P], start_row[0:1, :], start=True, stop=True)\
                        .then_inc(S["starts_wide"], 1)
                    group(k, 0, first=True)
                    with pe.Fori(1, GROUPS) as g:
                        group(k, g)
                    for w in range(W_STEPS):
                        weight_step(k, GROUPS, w)

                res = cols[1 - l]
                pe.wait_ge(S["relu"] if l == 0 else S["complete"], 2 if l == 0 else 1)
                for i in range(NK // 2):
                    if i >= 4:
                        if l == 0 and i % 2 == 0:
                            pe.wait_ge(S["back_a"], (i - 4) // 2 + 1)
                        elif l == 0:
                            pe.wait_ge(S["back_v"], (i - 4) // 2 + 1)
                        else:
                            pe.wait_ge(S["back_v"], i - 3)
                    for j in range(4):
                        k0, h = 2 * i + j // H, j % H
                        last = nc.tensor.transpose(bank[4 + i % 4][:P, j * 128:(j + 1) * 128],
                                                   strided_cols(res, h, k0, 1)[:, 0, :], ident[:, :])
                    last.then_inc(S["back"], 1)

            pe.wait_ge(L[1]["back_v"], NK // 2)
            turn_rows(5 * H, f_rows, NK)
            pe.wait_ge(turned_used, 2 * 5 * H)
            pe.wait_ge(gate_in, 2 * 16)
            for k in range(NK):
                for h in range(H):
                    last = nc.tensor.matmul(bank[2][:P, k * EXPERTS:(k + 1) * EXPERTS],
                                            strided_cols(cols[1], h, k, 1)[:, 0, :], gate_w[:, h, :],
                                            start=(h == 0), stop=(h == H - 1))
            last.then_inc(logits_done, 1)
            pe.wait_ge(totals_ready, 1)
            nc.tensor.matmul(bank[3][:P, 0:EXPERTS], tri[:, :], counts[:, :, NK - 1], start=True, stop=True)\
                .then_inc(before_ready, 1)

            def expert(pair, v):
                e = pair * 2 + v
                pe.wait_ge(slot_rows_in[v], pair * 16 + 16)
                for h in range(H):
                    pe.wait_ge(slot_cols_v if h == 0 else slot_cols_a, e + 1)
                    for j in range(SLOT_TILES):
                        last = nc.tensor.transpose(bank[4 + h][:, j * SLOT_TILE:(j + 1) * SLOT_TILE],
                                                   slot_rows[v][:, j, h * 128:(h + 1) * 128],
                                                   ident[0:SLOT_TILE, 0:SLOT_TILE])
                    last.then_inc(slots_turned, 1)
                pe.wait_ge(slot_cols_v, e + 2)
                pe.wait_ge(slot_cols_a, e + 2)
                pe.wait_ge(ew_in[v], pair * 32 + 32)
                for t in range(FT):
                    pe.wait_ge(mid_v if t % 2 else mid_a, e * (FT // 2) + (t // 2 + 1))
                    for h in range(H):
                        last = nc.tensor.matmul(bank[t % 4][:, 0:SLOTS], ew1[v][:, h, t * 128:(t + 1) * 128],
                                                slot_cols[v][:, h, :], start=(h == 0), stop=(h == H - 1))
                    last.then_inc(mid_done, 1)
                pe.wait_ge(mid_a, e * (FT // 2) + (FT // 2 + 2))
                pe.wait_ge(mid_v, e * (FT // 2) + (FT // 2 + 2))
                for j in range(SLOT_TILES):
                    pe.wait_ge(y_taken, e * SLOT_TILES + (j + 1))
                    for t in range(FT):
                        last = nc.tensor.matmul(bank[6 + j % 2][:SLOT_TILE, 0:D],
                                                hmid[v][:, t, j * SLOT_TILE:(j + 1) * SLOT_TILE], ew2[v][:, t, :],
                                                start=(t == 0), stop=(t == FT - 1))
                    last.then_inc(y_done, 1)

            with pe.Fori(0, EXPERTS // 2) as pair:
                for v in range(2):
                    expert(pair, v)

        @block.vector
        def _(dve):
            V = nc.vector
            for i in range(2):
                V.memset(cols[i][:, :, N:NPAD], 0.0)
            dve.wait_ge(edges_as_f, 1)
            V.tensor_reduce(spans[:, 0, :], edges_f[:, 0], AX.X, ALU.min)
            V.tensor_reduce(spans[:, 1, :], edges_f[:, 0], AX.X, ALU.max).then_inc(spans_done, 1)

            def layer_norm(nth, arrived):
                for k in range(NK):
                    arrived(k)
                    V.bn_stats(stats[:, k, :], x_rows[:, k, :])
                dve.drain()
                V.tensor_tensor(ln[:, 0, :], stats[:, :, 1], stats[:, :, 4], ALU.add)
                V.tensor_tensor(ln[:, 1, :], stats[:, :, 1], stats[:, :, 4], ALU.subtract)
                V.tensor_tensor(ln[:, 2, :], stats[:, :, 2], stats[:, :, 5], ALU.add)
                dve.drain()
                V.tensor_scalar(ln[:, 0, :], ln[:, 0, :], 0.5, None, ALU.mult)
                V.scalar_tensor_tensor(ln[:, 5, :], ln[:, 1, :], 0.25, ln[:, 1, :], ALU.mult, ALU.mult)
                V.tensor_scalar(ln[:, 2, :], ln[:, 2, :], 1.0 / D, EPS, ALU.mult, ALU.add)
                dve.drain()
                V.tensor_tensor(ln[:, 2, :], ln[:, 2, :], ln[:, 5, :], ALU.add).then_inc(var_ready, 1)
                dve.wait_ge(std_ready, nth)
                V.reciprocal(ln[:, 4, :], ln[:, 3, :])
                dve.drain()
                V.tensor_tensor(ln[:, 4, :], ln[:, 4, :], ln[:, 2, :], ALU.mult)
                dve.drain()
                V.tensor_tensor(ln[:, 4, :], ln[:, 4, :], ln[:, 3, :], ALU.add)
                dve.drain()
                V.tensor_scalar(ln[:, 4, :], ln[:, 4, :], 0.5, None, ALU.mult)
                dve.drain()
                V.reciprocal(ln[:, 4, :], ln[:, 4, :])
                dve.drain()
                for k in range(NK):
                    V.tensor_scalar(f_rows[:, k, :], x_rows[:, k, :], ln[:, 0, k:k + 1], ln[:, 4, k:k + 1],
                                    ALU.subtract, ALU.mult).then_inc(rows_ready, 1)

            layer_norm(1, lambda k: dve.wait_ge(x_in[k // 5], 16))

            dve.wait_ge(spans_turned, 1)
            V.tensor_copy(low, bank[0][0:1, 0:CHUNKS])

            def by_group(v):
                return v.rearrange("a (g c) -> a g c", c=GROUP_CHUNKS)

            def of_first(v):
                return by_group(v)[:, :, 0:1].to_broadcast([1, GROUPS, GROUP_CHUNKS])

            dve.drain()
            V.tensor_tensor(spread, bank[1][0:1, 0:CHUNKS], low, ALU.subtract)
            V.tensor_tensor(by_group(place_in_group), by_group(low), of_first(low), ALU.subtract)
            dve.drain()
            V.tensor_reduce(flag[:, 0:1], spread, AX.X, ALU.max)
            V.tensor_reduce(flag[:, 1:2], place_in_group, AX.X, ALU.max)
            V.tensor_reduce(flag[:, 2:3], place_in_group, AX.X, ALU.min)
            dve.drain()
            V.tensor_scalar(flag[:, 0:1], flag[:, 0:1], float(WIN - 1), None, ALU.is_le)
            V.tensor_scalar(flag[:, 1:2], flag[:, 1:2], float(GROUP_WIN - WIN), None, ALU.is_le)
            V.tensor_scalar(flag[:, 2:3], flag[:, 2:3], 0.0, None, ALU.is_ge)
            dve.drain()
            V.tensor_tensor(flag[:, 3:4], flag[:, 0:1], flag[:, 1:2], ALU.mult)
            dve.drain()
            one_pass = flag[:, 4:5]
            V.tensor_tensor(one_pass, flag[:, 3:4], flag[:, 2:3], ALU.mult)
            dve.drain()
            V.tensor_scalar(first_start, low, one_pass, None, ALU.mult)
            V.tensor_scalar(flag[:, 5:6], one_pass, float(-WIN), float(WIN), ALU.mult, ALU.add)
            V.tensor_scalar(passes_i[:, :], one_pass, float(1 - WINDOW_PASSES), float(WINDOW_PASSES),
                            ALU.mult, ALU.add).then_inc(passes_ready, 1)
            step, moved = flag[:, 5:6], flag[:, 6:7]

            for l in range(2):
                S = L[l]
                res = cols[1 - l]
                dve.sem_inc(S["added"], HOTS)
                dve.sem_inc(S["w_added"], H)
                V.memset(moved, 0.0)

                def windows(k):
                    dve.drain()
                    V.tensor_scalar(start_row[:, :], first_start, moved, None, ALU.add).then_inc(S["starts"], 1)
                    dve.drain()
                    V.tensor_tensor(moved, moved, step, ALU.add)
                    V.tensor_tensor(by_group(off_f[:, :]), by_group(start_row[:, :]), of_first(start_row[:, :]),
                                    ALU.subtract)
                    V.tensor_copy(base_i[:, :], by_group(start_row[:, :])[:, :, 0])
                    dve.drain()
                    V.tensor_copy(off_i[:, :], off_f[:, :])
                    dve.wait_ge(edges_copied, 3)
                    dve.wait_ge(S["starts_wide"], k + 1)
                    V.tensor_tensor(key_t[:, 0, :], edges_t[:, 0, :], bank[0][:P, 0:CHUNKS], ALU.subtract)
                    dve.drain()
                    V.tensor_tensor(key_t[:, 1, :], key_t[:, 0, :], edges_t[:, 1, :], ALU.add)
                    V.tensor_scalar(key_t[:, 2, :], key_t[:, 0, :], 0.0, None, ALU.is_ge)
                    dve.drain()
                    V.scalar_tensor_tensor(key_t[:, 2, :], key_t[:, 0, :], float(WIN), key_t[:, 2, :],
                                           ALU.is_lt, ALU.mult)
                    dve.drain()
                    V.tensor_tensor(key_t[:, 1, :], key_t[:, 1, :], key_t[:, 2, :], ALU.mult)
                    dve.drain()
                    V.tensor_scalar(key[:, :], key_t[:, 1, :], -1.0, None, ALU.add)
                    dve.drain()

                def one_hot(k, g, u):
                    dve.wait_ge(S["summed"], k * CHUNKS + g * GROUP_CHUNKS + (u + SUMMED_CREDIT - HOTS + 1))
                    V.tensor_scalar(hot[:, u % HOTS, :], key_iota[:, :], key[:, bass.ds(g * GROUP_CHUNKS + u, 1)],
                                    None, ALU.is_equal).then_inc(S["hot"], 1)

                def add_chunk(k, g, u):
                    off = dve.value_load(off_i[0:1, bass.ds(g * GROUP_CHUNKS + u, 1)], min_val=0,
                                         max_val=GROUP_WIN - WIN)
                    at = accum[:, bass.ds((g % 2) * SPAN, SPAN)].rearrange("c (h r n) -> c h r n", h=H, r=R)\
                        [:, :, :, bass.ds(off, WIN)]
                    dve.wait_ge(S["summed"], k * CHUNKS + g * GROUP_CHUNKS + (u + SUMMED_CREDIT + 1))
                    dve.wait_ge(S["added"], k * CHUNKS + g * GROUP_CHUNKS + (u + HOTS))
                    V.tensor_tensor(at, chunk_sum[u % HOTS].rearrange("c h (r n) -> c h r n", r=R), at, ALU.add)\
                        .then_inc(S["added"], 1)

                def add_weighted(k, g, ho):
                    base = dve.value_load(base_i[0:1, bass.ds(g - 1, 1)], min_val=0, max_val=NPAD - GROUP_WIN)
                    at = res[:, ho, bass.ds(base, GROUP_WIN)]
                    dve.wait_ge(S["w_done"], k * (GROUPS * H) + g * H + (ho + 3))
                    dve.wait_ge(S["w_added"], k * (GROUPS * H) + g * H + ho)
                    V.tensor_tensor(at, bank[2 + ho][:, 0:GROUP_WIN], at, ALU.add).then_inc(S["w_added"], 1)

                def group(k, g, first=False):
                    one_hot(k, g, 0)
                    one_hot(k, g, 1)
                    dve.wait_ge(S["zeroed"], k * GROUPS + g + 1)
                    for u in range(GROUP_CHUNKS):
                        if u + 2 < GROUP_CHUNKS:
                            one_hot(k, g, u + 2)
                        add_chunk(k, g, u)
                        if not first and u in (GROUP_CHUNKS // 2 + 4, GROUP_CHUNKS - 1):
                            add_weighted(k, g, int(u == GROUP_CHUNKS - 1))

                passes = passes_of(dve)
                dve.wait_ge(S["self_out"], SELF_BLOCKS * H)
                with dve.Fori(0, passes) as k:
                    windows(k)
                    group(k, 0, first=True)
                    with dve.Fori(1, GROUPS) as g:
                        group(k, g)
                    for ho in range(H):
                        add_weighted(k, GROUPS, ho)
                dve.drain().then_inc(S["complete"], 1)
                if l == 0:
                    V.tensor_scalar(res[:, 0, 0:N], res[:, 0, 0:N], 0.0, None, ALU.max).then_inc(S["relu"], 1)
                    for i in range(1, NK // 2, 2):
                        dve.wait_ge(S["back"], i + 1)
                        V.tensor_copy(f_rows[:, 2 * i:2 * i + 2, :],
                                      bank[4 + i % 4][:P, :].rearrange("p (k d) -> p k d", k=2))\
                            .then_inc(S["back_v"], 1)
                else:
                    for i in range(NK // 2):
                        dve.wait_ge(S["back"], i + 1)
                        V.tensor_tensor(x_rows[:, 2 * i:2 * i + 2, :], x_rows[:, 2 * i:2 * i + 2, :],
                                        bank[4 + i % 4][:P, :].rearrange("p (k d) -> p k d", k=2), ALU.add)\
                            .then_inc(S["back_v"], 1)

            layer_norm(2, lambda k: dve.wait_ge(L[1]["back_v"], k // 2 + 1))

            wide = [P, NK, EXPERTS]
            dve.wait_ge(logits_done, 1)
            dve.wait_ge(gate_in, 2 * 16)
            V.tensor_tensor(lg[:, 0], bank[2][:P, 0:NK * EXPERTS].rearrange("p (k e) -> p k e", k=NK),
                            gate_b[:, None, :].to_broadcast(wide), ALU.add)
            dve.drain()
            V.tensor_reduce(tok[:, 0, :], lg[:, 0], AX.X, ALU.max)
            dve.drain()
            V.tensor_tensor(lg[:, 0], lg[:, 0], tok[:, 0, :, None].to_broadcast(wide), ALU.subtract)\
                .then_inc(scores_ready, 1)
            dve.wait_ge(exps_ready, 1)
            V.tensor_reduce(tok[:, 1, :], lg[:, 1], AX.X, ALU.add)
            dve.drain()
            V.reciprocal(tok[:, 2, :], tok[:, 1, :])
            dve.drain()
            V.tensor_tensor(lg[:, 2], lg[:, 1], tok[:, 2, :, None].to_broadcast(wide), ALU.mult)
            dve.drain()
            best = tok[:, 3, :]
            V.tensor_reduce(best, lg[:, 2], AX.X, ALU.max)
            dve.drain()
            V.tensor_tensor(lg[:, 3], lg[:, 2], tok[:, 3, :, None].to_broadcast(wide), ALU.is_equal)
            dve.drain()
            V.scalar_tensor_tensor(lg[:, 0], e_iota[:, None, :].to_broadcast(wide), float(-EXPERTS), lg[:, 3],
                                   ALU.add, ALU.mult)
            dve.drain()
            V.tensor_reduce(tok[:, 4, :], lg[:, 0], AX.X, ALU.min)
            dve.drain()
            V.tensor_scalar(tok[:, 5, :], tok[:, 4, :], 0.0, float(-EXPERTS), ALU.is_equal, ALU.mult)
            dve.drain()
            V.tensor_tensor(tok[:, 4, :], tok[:, 4, :], tok[:, 5, :], ALU.add)
            dve.drain()
            for e in range(EXPERTS):
                V.tensor_scalar(picked[:, e, :], tok[:, 4, :], float(e - EXPERTS), None, ALU.is_equal)
            dve.drain()
            for e in range(EXPERTS):
                last = V.tensor_tensor_scan(counts[:, e, :], picked[:, e, :], zeros[:P, 0:NK], 0.0, ALU.add, ALU.add)
            last.then_inc(totals_ready, 1)
            dve.wait_ge(before_ready, 1)
            place = lg[:, 1].rearrange("p k e -> p (k e)").rearrange("p (e k) -> p e k", e=EXPERTS)
            V.tensor_tensor(place, counts[:, :, :],
                            bank[3][:P, 0:EXPERTS, None].to_broadcast([P, EXPERTS, NK]), ALU.add)
            dve.drain()
            V.tensor_tensor(place, place, picked[:, :, :], ALU.mult)
            dve.drain()
            V.tensor_reduce(tok[:, 5, :], place.rearrange("p e k -> p k e"), AX.X, ALU.add)
            dve.drain()
            kept = tok[:, 6, :]
            V.tensor_scalar(kept, tok[:, 5, :], float(CAP), None, ALU.is_le)
            V.scalar_tensor_tensor(tok[:, 7, :], tok[:, 4, :], float(SLOTS), tok[:, 5, :], ALU.mult, ALU.add)
            V.tensor_tensor(tok[:, 11, :], best, best, ALU.is_equal)
            dve.drain()
            V.tensor_scalar(tok[:, 7, :], tok[:, 7, :], float(EXPERTS * SLOTS - 1), None, ALU.add)
            V.tensor_scalar(tok[:, 9, :], kept, -8192.0, 8192.0, ALU.mult, ALU.add)
            V.tensor_tensor(tok[:, 10, :], kept, tok[:, 11, :], ALU.mult)
            V.memset(tok[:, 8, :], 0.0)
            dve.drain()
            V.tensor_copy(tok[:, 11, :].bitcast(I32), tok[:, 10, :])
            V.tensor_tensor(tok[:, 9, :], tok[:, 7, :], tok[:, 9, :], ALU.add)
            V.tensor_tensor(tok[:, 7, :], tok[:, 7, :], kept, ALU.mult)
            dve.drain()
            V.copy_predicated(tok[:, 8, :], tok[:, 11, :].bitcast(I32), best)
            V.tensor_copy(slot_from[:, :], tok[:, 7, :])
            V.tensor_copy(slot_to[:, :], tok[:, 9, :]).then_inc(slots_ready, 1)

            dve.sem_inc(slot_cols_v, 1)
            dve.sem_inc(slot_cols_a, 1)
            dve.sem_inc(mid_v, 2)
            dve.sem_inc(mid_a, 2)
            dve.sem_inc(y_taken, 2)
            dve.wait_ge(b2_in, 16)

            def expert(pair, v):
                e = pair * 2 + v
                dve.wait_ge(slots_turned, e * H + 1)
                V.tensor_copy(slot_cols[v][:, 0, :], bank[4][:, 0:SLOTS]).then_inc(slot_cols_v, 1)
                for t in range(1, FT, 2):
                    dve.wait_ge(mid_done, e * FT + (t + 1))
                    V.tensor_scalar(hmid[v][:, t, :], bank[t % 4][:, 0:SLOTS],
                                    bias_cols[:, bass.ds(e * FT + t, 1)], 0.0, ALU.add, ALU.max).then_inc(mid_v, 1)
                if not isinstance(pair, int):
                    dve.wait_ge(y_stored[v], pair * 16)
                for j in range(SLOT_TILES):
                    i = j % 2
                    finite, stand_in = y_rows[v][:, j, 0, :], y_rows[v][:, j, 1, :]
                    dve.wait_ge(y_done, e * SLOT_TILES + (j + 1))
                    V.tensor_tensor(y_raw[i], bank[6 + i][:SLOT_TILE, 0:D], b2[:, bass.ds(e, 1), :]
                                    .rearrange("p a d -> p (a d)"), ALU.add).then_inc(y_taken, 1)
                    V.memset(finite, 0.0)
                    dve.drain()
                    V.tensor_scalar(y_finite[:, i, :], y_raw[i], 0.0, 0.0, ALU.mult, ALU.is_equal)
                    V.tensor_scalar(y_over[i], y_raw[i], FLT_MAX, NAN_INF_TO, ALU.is_gt, ALU.mult)
                    V.tensor_scalar(y_under[i], y_raw[i], -FLT_MAX, NAN_INF_TO, ALU.is_lt, ALU.mult)
                    dve.drain()
                    V.copy_predicated(finite, y_finite[:, i, :], y_raw[i])
                    V.tensor_tensor(stand_in, y_over[i], y_under[i], ALU.subtract).then_inc(y_ready, 1)

            expert(0, 0)
            expert(0, 1)
            with dve.Fori(1, EXPERTS // 2) as pair:
                for v in range(2):
                    expert(pair, v)

            for k in range(NK):
                dve.wait_ge(y_in[k], 16)
                V.scalar_tensor_tensor(x_rows[:, k, :], y_tok[k][:, 0:D], tok[:, 8, k:k + 1], x_rows[:, k, :],
                                       ALU.mult, ALU.add)
                dve.drain()
                V.scalar_tensor_tensor(x_rows[:, k, :], y_tok[k][:, D:2 * D], tok[:, 10, k:k + 1], x_rows[:, k, :],
                                       ALU.mult, ALU.add).then_inc(out_ready, 1)


INPUTS = ["x", "src", "dst", "edge_type_8", "L0_gnn_W1", "L0_gnn_self_w1", "L0_gnn_b1", "L0_gnn_W2",
          "L0_gnn_self_w2", "L0_gnn_b2", "L0_ffn_gate_w", "L0_ffn_gate_b", "L0_ffn_w1", "L0_ffn_b1",
          "L0_ffn_w2", "L0_ffn_b2"]


SHAPES = {"x": (N, D), "src": (E,), "dst": (E,), "edge_type_8": (E,),
          "L0_ffn_gate_w": (D, EXPERTS), "L0_ffn_gate_b": (EXPERTS,), "L0_ffn_w1": (EXPERTS, D, FF),
          "L0_ffn_b1": (EXPERTS, FF), "L0_ffn_w2": (EXPERTS, FF, D), "L0_ffn_b2": (EXPERTS, D)}
for _l in "12":
    SHAPES |= {f"L0_gnn_W{_l}": (R, D, D), f"L0_gnn_self_w{_l}": (D, D), f"L0_gnn_b{_l}": (D,)}


def declare(nc):
    io = {n: nc.dram_tensor(f"in_{n}", SHAPES[n], I32 if n in ("src", "dst", "edge_type_8") else F32,
                            kind="ExternalInput").ap() for n in INPUTS}
    build(nc, io, nc.dram_tensor("out", (N, D), F32, kind="ExternalOutput").ap())


def kernel(**inputs):
    import concourse.bacc as bacc
    from concourse.bass_utils import run_bass_kernel_spmd

    nc = bacc.Bacc("TRN2", target_bir_lowering=False, num_devices=1)
    declare(nc)
    arrays = {f"in_{n}": np.ascontiguousarray(inputs[n]) for n in INPUTS}
    return run_bass_kernel_spmd(nc, [arrays], core_ids=[0]).results[0]["out"]
```

```python
from contextlib import ExitStack

import numpy as np
import concourse.bass as bass
from concourse import mybir

F32 = mybir.dt.float32
I32 = mybir.dt.int32
U32 = mybir.dt.uint32
ALU = mybir.AluOpType
ACT = mybir.ActivationFunctionType
AX = mybir.AxisListType

N, D, R, E = 2500, 256, 8, 40000
P = 125
NK = N // P
H = D // 128
TERMS = R + 1
CHUNKS = E // P
GROUP_CHUNKS = 16
GROUPS = CHUNKS // GROUP_CHUNKS
WIN = 16
KEYS = R * WIN
GROUP_WIN = 152
WINDOW_PASSES = -(-N // WIN)
NPAD = ((WINDOW_PASSES - 1) * WIN + GROUP_WIN + 127) // 128 * 128
EDGE_TILE, EDGE_TILES = 80, 4
RING = 16
HOTS = 8
OFFSETS = 8
SUMS = 4
STAGE = 8
STAGES = GROUP_CHUNKS // STAGE
SPAN = GROUP_WIN * R * H
SUMMED_CREDIT = RING + 1
ADDED_CREDIT = SUMMED_CREDIT + 1
W_STEPS = R * H * H
SELF_BLOCKS = 5
SELF_COLS = N // SELF_BLOCKS
EPS = 1e-5

EXPERTS, FF = 8, 1024
FT = FF // 128
CAP = -(-5 * N // (4 * EXPERTS))
SLOT_TILE, SLOT_TILES = 98, 4
SLOTS = SLOT_TILE * SLOT_TILES
assert RING == GROUP_CHUNKS and CAP <= SLOTS and GROUPS % 2 == 0 and RING % STAGE == 0 and GROUP_CHUNKS % RING == 0
B2_AT = EXPERTS * FT
GNN_AT = B2_AT + EXPERTS * H
BIASES = GNN_AT + 2 * H
NO_ROW = 8192
FLT_MAX = 3.4028234663852886e38
NAN_INF_TO = 10000.0


def w_steps_after(u):
    first, slots = 1, GROUP_CHUNKS - 3
    done = lambda v: min(W_STEPS, max(0, (v - first) * W_STEPS // slots))
    return range(done(u), done(u + 1))


def build(nc, io, out):
    with ExitStack() as ctx:
        def sb(name, shape, dt=F32):
            return ctx.enter_context(nc.sbuf_tensor(name, shape, dt))

        def sem(name):
            return ctx.enter_context(nc.semaphore(name))

        table = [nc.dram_tensor(f"table{l}", (N, D), F32, kind="Internal").ap() for l in range(2)]
        disp = nc.dram_tensor("dispatched", (EXPERTS * SLOTS, 2 * D), F32, kind="Internal").ap()
        slot_map = nc.dram_tensor("slot_map", (EXPERTS * SLOTS, 2), U32, kind="Internal").ap()

        rows = sb("rows", [P, NK, 2, D])
        f_rows, x_rows = rows[:, :, 0, :], rows[:, :, 1, :]
        cols = [sb(f"cols{i}", [128, H, NPAD]) for i in range(2)]
        accum = sb("accum", [128, 2 * SPAN])
        weights = [sb(f"weights{l}", [128, H, TERMS, D]) for l in range(2)]
        ring = sb("ring", [P, RING, D])
        hot = sb("hot", [P, HOTS, KEYS])
        ring_flat = ring[:, :, :].rearrange("p q d -> p (q d)")
        edges_i = ring_flat[:EDGE_TILE, 0:1500].bitcast(I32).rearrange("q (j t e) -> q j t e", j=3, t=EDGE_TILES)
        edges_f = ring_flat[:EDGE_TILE, 1500:3000].rearrange("q (j t e) -> q j t e", j=3, t=EDGE_TILES)
        edges_t = sb("edges_t", [P, 3, CHUNKS + GROUP_CHUNKS])
        spans = sb("spans", [EDGE_TILE, 2, EDGE_TILES])
        low, spread, place_in_group = (ring_flat[0:1, 3000 + i * CHUNKS:3000 + (i + 1) * CHUNKS] for i in range(3))
        first_start = sb("first_start", [1, CHUNKS])[:, :]
        flag = sb("flag", [1, 16])
        start_row = sb("start_row", [1, CHUNKS])
        off_f = sb("off_f", [1, CHUNKS])
        off_i = sb("off_i", [1, CHUNKS], I32)
        base_i = sb("base_i", [1, GROUPS], I32)
        passes_i = sb("passes_i", [1, 1], I32)
        key = sb("key", [P, CHUNKS + HOTS])
        key_t = sb("key_t", [P, 3, CHUNKS])
        stage = sb("stage", [P, STAGES, STAGE], U32)
        ident = sb("ident", [128, 128])
        tri = sb("tri", [P, P])
        ones = sb("ones", [1, 128])
        zeros = sb("zeros", [128, 4 * D])
        key_iota_i = sb("key_iota_i", [P, KEYS], I32)
        key_iota = sb("key_iota", [P, KEYS])
        e_iota_i = sb("e_iota_i", [P, EXPERTS], I32)
        e_iota = sb("e_iota", [P, EXPERTS])
        bias_rows = sb("bias_rows", [BIASES, 128])
        bias_cols = sb("bias_cols", [128, BIASES])
        stats = sb("stats", [P, NK, 6])
        ln = sb("ln", [P, 8, NK])
        gate_w = sb("gate_w", [128, H, EXPERTS])
        gate_b = sb("gate_b", [P, EXPERTS])
        lg = sb("lg", [P, 4, NK, EXPERTS])
        picked = sb("picked", [P, EXPERTS, NK])
        counts = sb("counts", [P, EXPERTS, NK])
        tok = sb("tok", [P, 12, NK])
        slot_to = sb("slot_to", [P, NK], U32)
        token_i = sb("token_i", [P, NK], I32)
        token_f = sb("token_f", [P, NK])
        token_info = sb("token_info", [P, NK, 2], U32)
        token_over = sb("token_over", [P, NK], U32)
        empty_info = sb("empty_info", [SLOT_TILE, EXPERTS * SLOT_TILES, 2], U32)
        slot_info = [sb(f"slot_info{v}", [SLOT_TILE, SLOT_TILES, 2], U32) for v in range(2)]
        y_finite = sb("y_finite", [SLOT_TILE, SLOT_TILES, D], mybir.dt.uint8)
        first_expert = sb("first_expert", [128, 4096])

        ew = [first_expert[:, :], accum[:, 0:4096]]
        ew1 = [w[:, 0:2048].rearrange("p (h f) -> p h f", h=H) for w in ew]
        ew2 = [w[:, 2048:4096].rearrange("p (t d) -> p t d", t=FT) for w in ew]
        cflat = [cols[i][:, :, :].rearrange("p h n -> p (h n)") for i in range(2)]
        hmid = [cflat[i][:, 0:FT * SLOTS].rearrange("p (t n) -> p t n", t=FT) for i in range(2)]
        wflat = [weights[i][:, :, :, :].rearrange("p h t d -> p (h t d)") for i in range(2)]

        def slot_tiles(flat, at):
            return flat[:SLOT_TILE, at:at + SLOT_TILES * D].rearrange("p (j d) -> p j d", j=SLOT_TILES)

        slot_rows = [slot_tiles(wflat[i], 0) for i in range(2)]
        slot_res = [slot_tiles(wflat[i], 1024) for i in range(2)]
        slot_cols = [wflat[i][:, 2048:2048 + H * SLOTS].rearrange("p (h n) -> p h n", h=H) for i in range(2)]
        y_cols = [wflat[i][:, 3072:3072 + H * SLOTS].rearrange("p (h n) -> p h n", h=H) for i in range(2)]
        y_raw = [slot_tiles(ring_flat, 1024 * i) for i in range(2)]
        y_out = [slot_tiles(ring_flat, 2048 + 1024 * i) for i in range(2)]
        y_over, y_under = slot_tiles(cflat[0], FT * SLOTS), slot_tiles(cflat[1], FT * SLOTS)

        bank = [ctx.enter_context(nc.psum_tensor(f"bank{i}", [128, 512], F32)) for i in range(8)]
        chunk_sum = [bank[4 + i][:, 0:H * KEYS].rearrange("p (h k) -> p h k", h=H) for i in range(SUMS)]

        edges_in, gate_in, bias_in = sem("edges_in"), sem("gate_in"), sem("bias_in")
        x_in = [sem(f"x_in{i}") for i in range(4)]
        weights_in = [sem("weights_in0"), sem("weights_in1")]
        consts = sem("consts")
        dve_consts = sem("dve_consts")
        edges_as_f, spans_done = sem("edges_as_f"), sem("spans_done")
        edges_turned, spans_turned = sem("edges_turned"), sem("spans_turned")
        edges_copied = sem("edges_copied")
        bias_turned, bias_copied = sem("bias_turned"), sem("bias_copied")
        var_ready, std_ready = sem("var_ready"), sem("std_ready")
        rows_ready = sem("rows_ready")
        rows_ready_p = sem("rows_ready_p")
        norm_ready = sem("norm_ready")
        turned, turned_used = sem("turned"), sem("turned_used")
        passes_ready = sem("passes_ready")
        clears_done = sem("clears_done")
        disp_zero, disp_in, map_in, over_out = sem("disp_zero"), sem("disp_in"), sem("map_in"), sem("over_out")
        L = []
        for l in range(2):
            s = lambda name: sem(f"{name}_{l}")
            L.append(dict(
                table_in=s("table_in"), rows_out=s("rows_out"), starts=s("starts"), starts_wide=s("starts_wide"),
                keyed=s("keyed"), staged=s("staged"), slot=[s(f"slot{q}") for q in range(RING)],
                hot=s("hot"), summed=s("summed"), added=s("added"), zeroed=s("zeroed"), w_done=s("w_done"),
                w_added=s("w_added"), self_done=s("self_done"), self_out=s("self_out"), cols_in=s("cols_in"),
                complete=s("complete"), relu=s("relu"), back=s("back"), back_a=s("back_a"), back_v=s("back_v"),
                claimed=s("claimed")))
        logits_done, scores_ready, exps_ready = sem("logits_done"), sem("scores_ready"), sem("exps_ready")
        totals_ready, before_ready = sem("totals_ready"), sem("before_ready")
        slots_ready, info_ready = sem("slots_ready"), sem("info_ready")
        pair = lambda name: [sem(f"{name}0"), sem(f"{name}1")]
        ew1_in, ew2_in, slot_rows_in, slot_res_in, info_in = map(
            pair, ("ew1_in", "ew2_in", "slot_rows_in", "slot_res_in", "info_in"))
        slots_turned, slot_cols_v, slot_cols_a = sem("slots_turned"), sem("slot_cols_v"), sem("slot_cols_a")
        mid_done, mid_a, mid_v = sem("mid_done"), sem("mid_a"), sem("mid_v")
        y_done, y_cols_in = sem("y_done"), sem("y_cols_in")
        y_turned, y_scaled, y_range, y_result, y_sent = (
            sem("y_turned"), sem("y_scaled"), sem("y_range"), sem("y_result"), pair("y_sent"))

        def passes_of(eng):
            eng.wait_ge(passes_ready, 1)
            return eng.value_load(passes_i[0:1, 0:1], min_val=1, max_val=WINDOW_PASSES)

        def strided_cols(buf, h, k0, nk):
            return buf[:, h, 0:N].rearrange("c (p k) -> c k p", k=NK)[:, k0:k0 + nk, :]

        block = ctx.enter_context(nc.Block())

        @block.sync
        def _(sp):
            x_v = io["x"].rearrange("(p k) d -> p k d", k=NK)
            for i in range(4):
                sp.dma_start(x_rows[:, 5 * i:5 * i + 5, :], x_v[:, 5 * i:5 * i + 5, :]).then_inc(x_in[i], 16)
            sp.dma_start(bias_rows[0:B2_AT, :], io["L0_ffn_b1"].rearrange("e (t c) -> (e t) c", c=128))\
              .then_inc(bias_in, 16)
            sp.dma_start(bias_rows[B2_AT:GNN_AT, :], io["L0_ffn_b2"].rearrange("e (h c) -> (e h) c", c=128))\
              .then_inc(bias_in, 16)
            for l in range(2):
                at = GNN_AT + H * l
                sp.dma_start(bias_rows[at:at + H, :], io[f"L0_gnn_b{l + 1}"].rearrange("(h c) -> h c", c=128))\
                  .then_inc(bias_in, 16)

            def load_weights(l):
                for h in range(H):
                    sp.dma_start(weights[l][:, h, 0:R, :],
                                 io[f"L0_gnn_W{l + 1}"][:, h * 128:h * 128 + 128, :].rearrange("r c o -> c r o"))\
                      .then_inc(weights_in[l], 16)
                    sp.dma_start(weights[l][:, h, R, :], io[f"L0_gnn_self_w{l + 1}"][h * 128:h * 128 + 128, :])\
                      .then_inc(weights_in[l], 16)

            t_v = table[0].rearrange("(p k) d -> p k d", k=NK)
            for i in range(5):
                sp.wait_ge(rows_ready, 3 * i + 3)
                sp.wait_ge(rows_ready_p, i + 1)
                sp.dma_start(t_v[:, 4 * i:4 * i + 4, :], f_rows[:, 4 * i:4 * i + 4, :]).then_inc(L[0]["table_in"], 16)
            load_weights(0)
            sp.wait_ge(consts, 1)
            for j in range(0, SLOT_TILES, 2):
                for e in range(EXPERTS):
                    sp.dma_start(disp[e * SLOTS:(e + 1) * SLOTS, :].rearrange("(p j) d -> p j d", j=SLOT_TILES)
                                 [:, j:j + 2, :], zeros[0:SLOT_TILE, :].rearrange("p (j d) -> p j d", j=2))\
                      .then_inc(disp_zero, 16)
            sp.dma_start(slot_map.rearrange("(p j) w -> p j w", p=SLOT_TILE), empty_info[:, :, :])\
              .then_inc(disp_zero, 16)
            load_weights(1)
            sp.dma_start(gate_w[:, :, :], io["L0_ffn_gate_w"].rearrange("(h c) e -> c h e", c=128)).then_inc(gate_in, 16)
            sp.dma_start(gate_b[:, :], io["L0_ffn_gate_b"].rearrange("(a e) -> a e", a=1).to_broadcast([P, EXPERTS]))\
              .then_inc(gate_in, 16)
            t_v = table[1].rearrange("(p k) d -> p k d", k=NK)
            for i in range(5):
                sp.wait_ge(L[0]["back_a"], i + 1)
                sp.wait_ge(L[0]["back_v"], i + 1)
                sp.dma_start(t_v[:, 4 * i:4 * i + 4, :], f_rows[:, 4 * i:4 * i + 4, :]).then_inc(L[1]["table_in"], 16)

            def load_w1(e, v):
                sp.dma_start(ew1[v], io["L0_ffn_w1"][bass.ds(e, 1), :, :].rearrange("a (h c) f -> c (a h) f", c=128))\
                  .then_inc(ew1_in[v], 16)

            def load_w2(e, v):
                sp.dma_start(ew2[v], io["L0_ffn_w2"][bass.ds(e, 1), :, :].rearrange("a (t c) d -> c (a t) d", c=128))\
                  .then_inc(ew2_in[v], 16)

            def slot_part(e, part):
                return disp[bass.ds(e * SLOTS, SLOTS), part * D:(part + 1) * D].rearrange(
                    "(p j) d -> p j d", j=SLOT_TILES)

            def load_info(e, v):
                sp.dma_start(slot_info[v][:, :, :], slot_map[bass.ds(e * SLOTS, SLOTS), :].rearrange(
                    "(p j) w -> p j w", j=SLOT_TILES)).then_inc(info_in[v], 16)

            load_w1(0, 0)
            load_w2(0, 0)
            sp.wait_ge(L[1]["complete"], 1)
            sp.wait_ge(clears_done, 1)
            load_w1(1, 1)
            load_w2(1, 1)
            sp.wait_ge(disp_in, NK * 16)
            for v in range(2):
                sp.dma_start(slot_rows[v], slot_part(v, 0)).then_inc(slot_rows_in[v], 16)
            for v in range(2):
                sp.dma_start(slot_res[v], slot_part(v, 1)).then_inc(slot_res_in[v], 16)
            sp.wait_ge(map_in, NK * 16)
            load_info(0, 0)
            load_info(1, 1)
            with sp.Fori(1, EXPERTS // 2) as half:
                for v in range(2):
                    e = half * 2 + v
                    sp.wait_ge(slots_turned, (e - 1) * H)
                    sp.dma_start(slot_rows[v], slot_part(e, 0)).then_inc(slot_rows_in[v], 16)
                    sp.wait_ge(mid_done, (e - 1) * FT)
                    load_w1(e, v)
                    sp.wait_ge(y_done, (e - 1) * H)
                    load_w2(e, v)
                    sp.wait_ge(y_result, e - 1)
                    sp.dma_start(slot_res[v], slot_part(e, 1)).then_inc(slot_res_in[v], 16)
                    sp.wait_ge(y_sent[v], half * (SLOT_TILES * 16))
                    load_info(e, v)

        @block.gpsimd
        def _(pool):
            pool.memset(zeros[:, :], 0.0)
            pool.memset(ident[:, :], 0.0)
            pool.memset(tri[:, :], 1.0)
            pool.memset(ones[:, :], 1.0)
            pool.memset(empty_info[:, :, 0:1], NO_ROW)
            pool.memset(empty_info[:, :, 1:2], 0)
            pool.iota(token_i[:, :], pattern=[[1, NK]], base=0, channel_multiplier=NK)
            pool.iota(key_iota_i[:, :], pattern=[[1, KEYS]], base=0, channel_multiplier=0)
            pool.iota(e_iota_i[:, :], pattern=[[1, EXPERTS]], base=0, channel_multiplier=0)
            pool.drain()
            pool.affine_select(out=ident[:, :], in_=ident[:, :], compare_op=ALU.not_equal, fill=1.0, base=0,
                               pattern=[[-1, 128]], channel_multiplier=1)
            pool.affine_select(out=tri[:, :], in_=tri[:, :], compare_op=ALU.is_gt, fill=0.0, base=0,
                               pattern=[[1, P]], channel_multiplier=-1)
            pool.tensor_copy(key_iota[:, :], key_iota_i[:, :])
            pool.tensor_copy(e_iota[:, :], e_iota_i[:, :])
            pool.tensor_copy(token_f[:, :], token_i[:, :])
            pool.drain().then_inc(consts, 1)

            def normalise(nth):
                pool.wait_ge(norm_ready, nth)
                for k in range(3, NK, 4):
                    pool.tensor_scalar(f_rows[:, k, :], x_rows[:, k, :], ln[:, 0, k:k + 1], ln[:, 4, k:k + 1],
                                       ALU.subtract, ALU.mult).then_inc(rows_ready_p, 1)

            normalise(1)

            for l in range(2):
                S = L[l]
                passes = passes_of(pool)
                with pool.Fori(0, passes) as k:
                    with pool.Fori(0, GROUPS) as g:
                        for u in range(GROUP_CHUNKS):
                            q = u % RING
                            if u % STAGE == 0:
                                pool.wait_ge(S["staged"], k * (GROUPS * STAGES) + g * STAGES + (u // STAGE + 1))
                                pool.wait_ge(S["summed"],
                                             k * CHUNKS + g * GROUP_CHUNKS + (u + STAGE + SUMMED_CREDIT - RING))
                                pool.sem_inc(S["claimed"], 1)
                                pool.wait_ge(S["table_in"], 5 * 16)
                            pool.indirect_dma_start(
                                ring[:, q, :], None, table[l],
                                bass.IndirectOffsetOnAxis(ap=stage[:, u // STAGE, u % STAGE:u % STAGE + 1], axis=0),
                            ).then_inc(S["slot"][q], 16)

            normalise(2)

            def to_slots(dest, source, done):
                for k in range(NK):
                    pool.indirect_dma_start(
                        dest, bass.IndirectOffsetOnAxis(ap=slot_to[:, k:k + 1], axis=0), source(k), None,
                        bounds_check=EXPERTS * SLOTS - 1, oob_is_err=False).then_inc(done, 16)

            pool.wait_ge(disp_zero, (2 * EXPERTS + 1) * 16)
            pool.wait_ge(slots_ready, 1)
            to_slots(disp, lambda k: rows[:, k, :, :].rearrange("p s d -> p (s d)"), disp_in)
            pool.wait_ge(info_ready, 1)
            to_slots(slot_map, lambda k: token_info[:, k, :], map_in)
            for k in range(NK):
                pool.indirect_dma_start(
                    out, bass.IndirectOffsetOnAxis(ap=token_over[:, k:k + 1], axis=0), x_rows[:, k, :], None,
                    bounds_check=N - 1, oob_is_err=False).then_inc(over_out, 16)

            def send(half, v):
                e = half * 2 + v
                pool.wait_ge(y_scaled, e * SLOT_TILES + SLOT_TILES)
                pool.sem_inc(L[1]["claimed"], 1)
                pool.tensor_scalar(y_over, y_raw[v], FLT_MAX, NAN_INF_TO, ALU.is_gt, ALU.mult)
                pool.tensor_scalar(y_under, y_raw[v], -FLT_MAX, -NAN_INF_TO, ALU.is_lt, ALU.mult)\
                    .then_inc(y_range, 1)
                pool.wait_ge(y_result, e + 1)
                pool.sem_inc(L[1]["claimed"], 1)
                pool.wait_ge(map_in, NK * 16)
                for j in range(SLOT_TILES):
                    pool.indirect_dma_start(
                        out, bass.IndirectOffsetOnAxis(ap=slot_info[v][:, j, 0:1], axis=0), y_out[v][:, j, :], None,
                        bounds_check=N - 1, oob_is_err=False).then_inc(y_sent[v], 16)

            with pool.Fori(0, EXPERTS // 2) as half:
                for v in range(2):
                    send(half, v)
            pool.wait_ge(over_out, NK * 16)
            for v in range(2):
                pool.wait_ge(y_sent[v], EXPERTS // 2 * SLOT_TILES * 16)

        @block.scalar
        def _(act):
            for j, name in enumerate(("dst", "edge_type_8", "src")):
                act.dma_start(edges_i[:, j, :, :],
                              io[name].rearrange("(t q e) -> q t e", q=EDGE_TILE, e=P)).then_inc(edges_in, 16)
            act.wait_ge(edges_in, 3 * 16)
            for j in range(3):
                nc.scalar.activation(edges_f[:, j], edges_i[:, j], ACT.Copy).then_inc(edges_as_f, 1)
            act.wait_ge(edges_turned, 3)
            nc.scalar.activation(edges_t[:, 0, 0:CHUNKS], bank[4][:P, 0:CHUNKS], ACT.Copy).then_inc(edges_copied, 1)
            nc.scalar.activation(edges_t[:, 1, 0:CHUNKS], bank[5][:P, 0:CHUNKS], ACT.Copy, scale=float(WIN), bias=1.0)\
                .then_inc(edges_copied, 1)
            nc.scalar.activation(edges_t[:, 2, CHUNKS:], bank[6][:P, 0:GROUP_CHUNKS], ACT.Copy)
            nc.scalar.activation(edges_t[:, 2, 0:CHUNKS], bank[6][:P, 0:CHUNKS], ACT.Copy).then_inc(edges_copied, 1)
            act.drain()

            def stage_indices(l, c, s):
                nc.scalar.activation(stage[:, s, :], edges_t[:, 2, bass.ds(c, STAGE)], ACT.Copy)\
                    .then_inc(L[l]["staged"], 1)

            def clear_accum(l, odd):
                nc.scalar.activation(
                    accum[:, bass.ds(odd * SPAN, SPAN)].rearrange("c (a b) -> c a b", b=GROUP_WIN),
                    zeros[:, None, 0:GROUP_WIN].to_broadcast([128, R * H, GROUP_WIN]), ACT.Copy)\
                    .then_inc(L[l]["zeroed"], 1)

            for s in range(STAGES):
                stage_indices(0, s * STAGE, s)
            act.wait_ge(consts, 1)
            clear_accum(0, 0)
            act.wait_ge(bias_turned, 1)
            nc.scalar.activation(bias_cols[:, :], bank[3][:, 0:BIASES], ACT.Copy)\
                .then_inc(bias_copied, 1)
            act.wait_ge(var_ready, 1)
            nc.scalar.activation(ln[:, 3, :], ln[:, 2, :], ACT.Sqrt).then_inc(std_ready, 1)

            def turned_out(first, count, per, dest):
                for i in range(count):
                    act.wait_ge(turned, first + i + 1)
                    nc.scalar.activation(dest(i), bank[4 + (first + i) % 4][:, 0:4 * per]
                                         .rearrange("c (k p) -> c k p", k=4), ACT.Copy).then_inc(turned_used, 1)

            def dest_cols(buf):
                return lambda i: strided_cols(buf, i % H, 4 * (i // H), 4)

            turned_out(0, 5 * H, P, dest_cols(cols[0]))

            for l in range(2):
                S = L[l]
                act.wait_ge(bias_copied, 1)
                at = GNN_AT + H * l
                for i in range(SELF_BLOCKS * H):
                    b, h = i // H, i % H
                    act.wait_ge(S["self_done"], i + 1)
                    nc.scalar.activation(cols[1 - l][:, h, b * SELF_COLS:(b + 1) * SELF_COLS],
                                         bank[4 + i % 4][:, 0:SELF_COLS], ACT.Identity,
                                         bias=bias_cols[:, at + h:at + h + 1]).then_inc(S["self_out"], 1)

                passes = passes_of(act)
                with act.Fori(0, passes) as k:
                    with act.Fori(0, GROUPS) as g:
                        for s in range(STAGES):
                            act.wait_ge(S["slot"][(s + 1) * STAGE - 1], k * (GROUPS * 16) + g * 16 + 16)
                            stage_indices(l, g * GROUP_CHUNKS + (GROUP_CHUNKS + s * STAGE), s)
                        act.wait_ge(S["w_done"], k * (GROUPS * H) + g * H + 2 * H)
                        clear_accum(l, (g + 1) % 2)
                if l == 0:
                    for i in range(0, NK // 2, 2):
                        act.wait_ge(S["back"], i + 1)
                        nc.scalar.activation(f_rows[:, 2 * i:2 * i + 2, :],
                                             bank[4 + i % 4][:P, :].rearrange("p (k d) -> p k d", k=2), ACT.Relu)\
                            .then_inc(S["back_a"], 1)
                    for s in range(STAGES):
                        stage_indices(1, s * STAGE, s)
                    clear_accum(1, 0)
                    act.wait_ge(S["back"], NK // 2)
                    nc.scalar.activation(cols[1][:, 1, 0:N], cols[1][:, 1, 0:N], ACT.Relu).then_inc(S["relu"], 1)

            act.drain().then_inc(clears_done, 1)

            act.wait_ge(var_ready, 2)
            nc.scalar.activation(ln[:, 3, :], ln[:, 2, :], ACT.Sqrt).then_inc(std_ready, 1)
            turned_out(5 * H, 5 * H, P, dest_cols(cols[1]))
            act.wait_ge(scores_ready, 1)
            nc.scalar.activation(lg[:, 1], lg[:, 0], ACT.Exp).then_inc(exps_ready, 1)

            def expert(half, v, first):
                e = half * 2 + v
                act.wait_ge(slots_turned, e * H + 2)
                nc.scalar.activation(slot_cols[v][:, 1, :], bank[5][:, 0:SLOTS], ACT.Copy).then_inc(slot_cols_a, 1)
                for t in range(0, FT, 2):
                    act.wait_ge(mid_done, e * FT + (t + 1))
                    nc.scalar.activation(hmid[v][:, t, :], bank[0][:, 0:SLOTS], ACT.Relu,
                                         bias=bias_cols[:, bass.ds(e * FT + t, 1)]).then_inc(mid_a, 1)
                if not first:
                    scale(half - (1 - v), 1 - v)
                for h in range(H):
                    act.wait_ge(y_done, e * H + (h + 1))
                    nc.scalar.activation(y_cols[v][:, h, :], bank[6 + h][:, 0:SLOTS], ACT.Identity,
                                         bias=bias_cols[:, bass.ds(B2_AT + e * H + h, 1)]).then_inc(y_cols_in, 1)

            def scale(half, v):
                e = half * 2 + v
                act.wait_ge(info_in[v], half * 16 + 16)
                for j in range(SLOT_TILES):
                    act.wait_ge(y_turned, e * 2 + (j // 2 + 1))
                    nc.scalar.activation(y_raw[v][:, j, :], bank[2 + j // 2][:SLOT_TILE, j % 2 * D:(j % 2 + 1) * D],
                                         ACT.Copy, scale=slot_info[v][:, j, 1:2].bitcast(F32)).then_inc(y_scaled, 1)

            expert(0, 0, True)
            expert(0, 1, False)
            with act.Fori(1, EXPERTS // 2) as half:
                for v in range(2):
                    expert(half, v, False)
            scale(EXPERTS // 2 - 1, 1)

        @block.tensor
        def _(pe):
            pe.wait_ge(consts, 1)
            for j in range(3):
                pe.wait_ge(edges_as_f, j + 1)
                for t in range(EDGE_TILES):
                    last = nc.tensor.transpose(bank[4 + j][:P, t * EDGE_TILE:(t + 1) * EDGE_TILE], edges_f[:, j, t, :],
                                               ident[0:EDGE_TILE, 0:EDGE_TILE])
                last.then_inc(edges_turned, 1)
            pe.wait_ge(spans_done, 1)
            for m in range(2):
                for t in range(EDGE_TILES):
                    last = nc.tensor.matmul(bank[m][0:1, t * EDGE_TILE:(t + 1) * EDGE_TILE], spans[:, m, t:t + 1],
                                            ident[0:EDGE_TILE, 0:EDGE_TILE], start=True, stop=True)
            last.then_inc(spans_turned, 1)
            pe.wait_ge(bias_in, 4 * 16)
            nc.tensor.transpose(bank[3][:, 0:BIASES], bias_rows[:, :], ident[0:BIASES, 0:BIASES])\
                .then_inc(bias_turned, 1)

            def turn_rows(first, rows, ready):
                for i in range(5 * H):
                    k0, h, n = 4 * (i // H), i % H, first + i
                    pe.wait_ge(rows_ready, ready * (NK // 4 * 3) + k0 // 4 * 3 + 3)
                    pe.wait_ge(rows_ready_p, ready * (NK // 4) + k0 // 4 + 1)
                    if i >= 4:
                        pe.wait_ge(turned_used, n - 3)
                    for j in range(4):
                        last = nc.tensor.transpose(bank[4 + n % 4][:, j * P:(j + 1) * P],
                                                   rows[:, k0 + j, h * 128:(h + 1) * 128], ident[0:P, 0:P])
                    last.then_inc(turned, 1)

            pe.wait_ge(edges_copied, 3)
            turn_rows(0, f_rows, 0)

            for l in range(2):
                S = L[l]
                pe.sem_inc(S["summed"], SUMMED_CREDIT)
                pe.sem_inc(S["w_done"], 2 * H)
                feats = cols[l]
                if l == 0:
                    pe.wait_ge(turned_used, 5 * H)
                else:
                    pe.wait_ge(L[0]["relu"], 2)
                    pe.wait_ge(L[0]["back_a"], 5)
                    pe.wait_ge(L[0]["back_v"], 5)
                pe.wait_ge(weights_in[l], 2 * H * 16)
                for i in range(SELF_BLOCKS * H):
                    b, ho = i // H, i % H
                    if i >= 4:
                        pe.wait_ge(S["self_out"], i - 3)
                    for h in range(H):
                        last = nc.tensor.matmul(bank[4 + i % 4][:, 0:SELF_COLS],
                                                weights[l][:, h, R, ho * 128:(ho + 1) * 128],
                                                feats[:, h, b * SELF_COLS:(b + 1) * SELF_COLS],
                                                start=(h == 0), stop=(h == H - 1))
                    last.then_inc(S["self_done"], 1)
                pe.wait_ge(S["self_out"], SELF_BLOCKS * H)

                def weight_step(k, g, w):
                    ho, r, h = w // (R * H), w % (R * H) // H, w % H
                    if w == 0:
                        pe.wait_ge(S["added"], k * CHUNKS + g * GROUP_CHUNKS + ADDED_CREDIT)
                    if r == h == 0:
                        pe.wait_ge(S["w_added"], k * (GROUPS * H) + (g - 1) * H + (ho + 1))
                    at = ((g - 1) % 2) * SPAN + (h * R + r) * GROUP_WIN
                    ins = nc.tensor.matmul(bank[2 + ho][:, 0:GROUP_WIN], weights[l][:, h, r, ho * 128:(ho + 1) * 128],
                                           accum[:, bass.ds(at, GROUP_WIN)],
                                           start=(r == h == 0), stop=(w % (R * H) == R * H - 1))
                    if w % (R * H) == R * H - 1:
                        ins.then_inc(S["w_done"], 1)

                def group(k, g, first=False):
                    chunks = pe.snap(k * CHUNKS + g * GROUP_CHUNKS)
                    hots = pe.snap(k * (CHUNKS + HOTS) + g * GROUP_CHUNKS)
                    gathers = pe.snap(k * (GROUPS * 16) + g * 16)
                    for u in range(GROUP_CHUNKS):
                        q = u % RING
                        pe.wait_ge(S["slot"][q], gathers + 16)
                        pe.wait_ge(S["hot"], hots + (u + 1))
                        pe.wait_ge(S["added"], chunks + (u + ADDED_CREDIT - SUMS + 1))
                        for h in range(H):
                            last = nc.tensor.matmul(chunk_sum[u % SUMS][:, h, :], ring[:, q, h * 128:(h + 1) * 128],
                                                    hot[:, u % HOTS, :], start=True, stop=True)
                        last.then_inc(S["summed"], 1)
                        if not first:
                            for w in w_steps_after(u):
                                weight_step(k, g, w)

                passes = passes_of(pe)
                with pe.Fori(0, passes) as k:
                    pe.wait_ge(S["starts"], k + 1)
                    nc.tensor.matmul(bank[0][:P, 0:CHUNKS], ones[0:1, 0:P], start_row[0:1, :], start=True, stop=True)\
                        .then_inc(S["starts_wide"], 1)
                    group(k, 0, first=True)
                    with pe.Fori(1, GROUPS) as g:
                        group(k, g)
                    for w in range(W_STEPS):
                        weight_step(k, GROUPS, w)

                res = cols[1 - l]
                pe.wait_ge(S["complete"], 1)
                for i in range(NK // 2):
                    if i >= 4:
                        if l == 0 and i % 2 == 0:
                            pe.wait_ge(S["back_a"], (i - 4) // 2 + 1)
                        elif l == 0:
                            pe.wait_ge(S["back_v"], (i - 4) // 2 + 1)
                        else:
                            pe.wait_ge(S["back_v"], i - 3)
                    for j in range(4):
                        k0, h = 2 * i + j // H, j % H
                        last = nc.tensor.transpose(bank[4 + i % 4][:P, j * 128:(j + 1) * 128],
                                                   strided_cols(res, h, k0, 1)[:, 0, :], ident[:, :])
                    last.then_inc(S["back"], 1)

            pe.wait_ge(L[1]["back_v"], NK // 2)
            turn_rows(5 * H, f_rows, 1)
            pe.wait_ge(turned_used, 2 * 5 * H)
            pe.wait_ge(gate_in, 2 * 16)
            for k in range(NK):
                for h in range(H):
                    last = nc.tensor.matmul(bank[2][:P, k * EXPERTS:(k + 1) * EXPERTS],
                                            strided_cols(cols[1], h, k, 1)[:, 0, :], gate_w[:, h, :],
                                            start=(h == 0), stop=(h == H - 1))
            last.then_inc(logits_done, 1)
            pe.wait_ge(totals_ready, 1)
            nc.tensor.matmul(bank[3][:P, 0:EXPERTS], tri[:, :], counts[:, :, NK - 1], start=True, stop=True)\
                .then_inc(before_ready, 1)

            def turn_slots(half, v):
                e = half * 2 + v
                pe.wait_ge(slot_rows_in[v], half * 16 + 16)
                for h in range(H):
                    pe.wait_ge(slot_cols_a if h else slot_cols_v, e + 1)
                    for j in range(SLOT_TILES):
                        last = nc.tensor.transpose(bank[4 + h][:, j * SLOT_TILE:(j + 1) * SLOT_TILE],
                                                   slot_rows[v][:, j, h * 128:(h + 1) * 128],
                                                   ident[0:SLOT_TILE, 0:SLOT_TILE])
                    last.then_inc(slots_turned, 1)

            def turn_back(half, v):
                e = half * 2 + v
                pe.wait_ge(y_cols_in, e * H + H)
                if not (isinstance(e, int) and e == 0):
                    pe.wait_ge(y_scaled, e * SLOT_TILES)
                for j in range(SLOT_TILES):
                    for h in range(H):
                        at = j % 2 * D + h * 128
                        last = nc.tensor.transpose(bank[2 + j // 2][:SLOT_TILE, at:at + 128],
                                                   y_cols[v][:, h, j * SLOT_TILE:(j + 1) * SLOT_TILE], ident[:, :])
                    if j % 2:
                        last.then_inc(y_turned, 1)

            def expert(half, v, first=False, last_one=False):
                e = half * 2 + v
                pe.wait_ge(slot_cols_v, e + 2)
                pe.wait_ge(slot_cols_a, e + 2)
                pe.wait_ge(ew1_in[v], half * 16 + 16)
                for t in range(FT):
                    pe.wait_ge(mid_v if t % 2 else mid_a, e * (FT // 2) + (t // 2 + 1))
                    for h in range(H):
                        last = nc.tensor.matmul(bank[t % 2][:, 0:SLOTS], ew1[v][:, h, t * 128:(t + 1) * 128],
                                                slot_cols[v][:, h, :], start=(h == 0), stop=(h == H - 1))
                    last.then_inc(mid_done, 1)
                if not first:
                    turn_back(half - (1 - v), 1 - v)
                if not last_one:
                    turn_slots(half + v, 1 - v)
                pe.wait_ge(mid_a, e * (FT // 2) + (FT // 2 + 1))
                pe.wait_ge(mid_v, e * (FT // 2) + (FT // 2 + 1))
                pe.wait_ge(ew2_in[v], half * 16 + 16)
                for ho in range(H):
                    if not first:
                        pe.wait_ge(y_cols_in, e * H)
                    for t in range(FT):
                        last = nc.tensor.matmul(bank[6 + ho][:, 0:SLOTS], ew2[v][:, t, ho * 128:(ho + 1) * 128],
                                                hmid[v][:, t, :], start=(t == 0), stop=(t == FT - 1))
                    last.then_inc(y_done, 1)

            turn_slots(0, 0)
            expert(0, 0, first=True)
            expert(0, 1)
            with pe.Fori(1, EXPERTS // 2 - 1) as half:
                for v in range(2):
                    expert(half, v)
            expert(EXPERTS // 2 - 1, 0)
            expert(EXPERTS // 2 - 1, 1, last_one=True)
            turn_back(EXPERTS // 2 - 1, 1)

        @block.vector
        def _(dve):
            V = nc.vector
            off_regs = [dve.alloc_register(f"off{i}") for i in range(OFFSETS)]
            V.memset(key[:, CHUNKS:], -1.0)
            for i in range(2):
                V.memset(cols[i][:, :, N:NPAD], 0.0)
            dve.wait_ge(edges_as_f, 1)
            V.tensor_reduce(spans[:, 0, :], edges_f[:, 0], AX.X, ALU.min)
            V.tensor_reduce(spans[:, 1, :], edges_f[:, 0], AX.X, ALU.max).then_inc(spans_done, 1)

            def layer_norm(nth, arrived):
                for k in range(NK):
                    arrived(k)
                    V.bn_stats(stats[:, k, :], x_rows[:, k, :])
                dve.drain()
                V.tensor_tensor(ln[:, 0, :], stats[:, :, 1], stats[:, :, 4], ALU.add)
                V.tensor_tensor(ln[:, 1, :], stats[:, :, 1], stats[:, :, 4], ALU.subtract)
                V.tensor_tensor(ln[:, 2, :], stats[:, :, 2], stats[:, :, 5], ALU.add)
                dve.drain()
                V.tensor_scalar(ln[:, 0, :], ln[:, 0, :], 0.5, None, ALU.mult)
                V.scalar_tensor_tensor(ln[:, 5, :], ln[:, 1, :], 0.25, ln[:, 1, :], ALU.mult, ALU.mult)
                V.tensor_scalar(ln[:, 2, :], ln[:, 2, :], 1.0 / D, EPS, ALU.mult, ALU.add)
                dve.drain()
                V.tensor_tensor(ln[:, 2, :], ln[:, 2, :], ln[:, 5, :], ALU.add).then_inc(var_ready, 1)
                dve.wait_ge(std_ready, nth)
                V.reciprocal(ln[:, 4, :], ln[:, 3, :])
                dve.drain()
                V.tensor_tensor(ln[:, 4, :], ln[:, 4, :], ln[:, 2, :], ALU.mult)
                dve.drain()
                V.tensor_tensor(ln[:, 4, :], ln[:, 4, :], ln[:, 3, :], ALU.add)
                dve.drain()
                V.tensor_scalar(ln[:, 4, :], ln[:, 4, :], 0.5, None, ALU.mult)
                dve.drain()
                V.reciprocal(ln[:, 4, :], ln[:, 4, :])
                dve.drain().then_inc(norm_ready, 1)
                for k in range(NK):
                    if k % 4 != 3:
                        V.tensor_scalar(f_rows[:, k, :], x_rows[:, k, :], ln[:, 0, k:k + 1], ln[:, 4, k:k + 1],
                                        ALU.subtract, ALU.mult).then_inc(rows_ready, 1)

            layer_norm(1, lambda k: dve.wait_ge(x_in[k // 5], 16))

            dve.wait_ge(spans_turned, 1)
            V.tensor_copy(low, bank[0][0:1, 0:CHUNKS])

            def by_group(v):
                return v.rearrange("a (g c) -> a g c", c=GROUP_CHUNKS)

            def of_first(v):
                return by_group(v)[:, :, 0:1].to_broadcast([1, GROUPS, GROUP_CHUNKS])

            dve.drain()
            V.tensor_tensor(spread, bank[1][0:1, 0:CHUNKS], low, ALU.subtract)
            V.tensor_tensor(by_group(place_in_group), by_group(low), of_first(low), ALU.subtract)
            dve.drain()
            V.tensor_reduce(flag[:, 0:1], spread, AX.X, ALU.max)
            V.tensor_reduce(flag[:, 1:2], place_in_group, AX.X, ALU.max)
            V.tensor_reduce(flag[:, 2:3], place_in_group, AX.X, ALU.min)
            dve.drain()
            V.tensor_scalar(flag[:, 0:1], flag[:, 0:1], float(WIN - 1), None, ALU.is_le)
            V.tensor_scalar(flag[:, 1:2], flag[:, 1:2], float(GROUP_WIN - WIN), None, ALU.is_le)
            V.tensor_scalar(flag[:, 2:3], flag[:, 2:3], 0.0, None, ALU.is_ge)
            dve.drain()
            V.tensor_tensor(flag[:, 3:4], flag[:, 0:1], flag[:, 1:2], ALU.mult)
            dve.drain()
            one_pass = flag[:, 4:5]
            V.tensor_tensor(one_pass, flag[:, 3:4], flag[:, 2:3], ALU.mult)
            dve.drain()
            V.tensor_scalar(first_start, low, one_pass, None, ALU.mult)
            V.tensor_scalar(flag[:, 5:6], one_pass, float(-WIN), float(WIN), ALU.mult, ALU.add)
            V.tensor_scalar(passes_i[:, :], one_pass, float(1 - WINDOW_PASSES), float(WINDOW_PASSES),
                            ALU.mult, ALU.add).then_inc(passes_ready, 1)
            step, moved = flag[:, 5:6], flag[:, 6:7]

            for l in range(2):
                S = L[l]
                res = cols[1 - l]
                dve.sem_inc(S["added"], ADDED_CREDIT)
                dve.sem_inc(S["w_added"], H)
                V.memset(moved, 0.0)

                def windows(k):
                    dve.drain()
                    V.tensor_scalar(start_row[:, :], first_start, moved, None, ALU.add).then_inc(S["starts"], 1)
                    dve.drain()
                    V.tensor_tensor(moved, moved, step, ALU.add)
                    V.tensor_tensor(by_group(off_f[:, :]), by_group(start_row[:, :]), of_first(start_row[:, :]),
                                    ALU.subtract)
                    V.tensor_copy(base_i[:, :], by_group(start_row[:, :])[:, :, 0])
                    dve.drain()
                    V.tensor_copy(off_i[:, :], off_f[:, :])
                    dve.wait_ge(edges_copied, 3)
                    dve.wait_ge(S["starts_wide"], k + 1)
                    V.tensor_tensor(key_t[:, 0, :], edges_t[:, 0, 0:CHUNKS], bank[0][:P, 0:CHUNKS], ALU.subtract)
                    dve.drain()
                    V.tensor_tensor(key_t[:, 1, :], key_t[:, 0, :], edges_t[:, 1, 0:CHUNKS], ALU.add)
                    V.tensor_scalar(key_t[:, 2, :], key_t[:, 0, :], 0.0, None, ALU.is_ge)
                    dve.drain()
                    V.scalar_tensor_tensor(key_t[:, 2, :], key_t[:, 0, :], float(WIN), key_t[:, 2, :],
                                           ALU.is_lt, ALU.mult)
                    dve.drain()
                    V.tensor_tensor(key_t[:, 1, :], key_t[:, 1, :], key_t[:, 2, :], ALU.mult)
                    dve.drain()
                    V.tensor_scalar(key[:, 0:CHUNKS], key_t[:, 1, :], -1.0, None, ALU.add)
                    dve.drain()

                def one_hot(c, u):
                    V.tensor_scalar(hot[:, u % HOTS, :], key_iota[:, :], key[:, bass.ds(c, 1)],
                                    None, ALU.is_equal).then_inc(S["hot"], 1)

                def add_chunk(chunks, buf, off, u):
                    at = accum[:, bass.ds(buf, SPAN)].rearrange("c (h r n) -> c h r n", h=H, r=R)\
                        [:, :, :, bass.ds(off, WIN)]
                    dve.wait_ge(S["summed"], chunks + (u + SUMMED_CREDIT + 1))
                    dve.wait_ge(S["added"], chunks + (u + ADDED_CREDIT))
                    V.tensor_tensor(at, chunk_sum[u % SUMS].rearrange("c h (r n) -> c h r n", r=R), at, ALU.add)\
                        .then_inc(S["added"], 1)

                def add_weighted(k, g, ho):
                    base = dve.value_load(base_i[0:1, bass.ds(g - 1, 1)], min_val=0, max_val=NPAD - GROUP_WIN)
                    at = res[:, ho, bass.ds(base, GROUP_WIN)]
                    dve.wait_ge(S["w_done"], k * (GROUPS * H) + g * H + (ho + 3))
                    dve.wait_ge(S["w_added"], k * (GROUPS * H) + g * H + ho)
                    V.tensor_tensor(at, bank[2 + ho][:, 0:GROUP_WIN], at, ALU.add).then_inc(S["w_added"], 1)

                def group(k, g, first=False):
                    chunks = dve.snap(k * CHUNKS + g * GROUP_CHUNKS)
                    column = dve.snap(g * GROUP_CHUNKS)
                    buf = dve.snap((g % 2) * SPAN)
                    for u in range(GROUP_CHUNKS):
                        if u % OFFSETS == 0:
                            dve.load(off_regs, off_i[0:1, bass.ds(column + u, OFFSETS)])
                            offs = [dve.snap(r, min_val=0, max_val=GROUP_WIN - WIN) for r in off_regs]
                        if u == 0:
                            dve.wait_ge(S["zeroed"], k * GROUPS + g + 1)
                        add_chunk(chunks, buf, offs[u % OFFSETS], u)
                        one_hot(column + (u + HOTS), u)
                        if not first and u in (GROUP_CHUNKS // 2 + 1, GROUP_CHUNKS - 1):
                            add_weighted(k, g, int(u == GROUP_CHUNKS - 1))

                passes = passes_of(dve)
                dve.wait_ge(S["self_out"], SELF_BLOCKS * H)
                with dve.Fori(0, passes) as k:
                    windows(k)
                    for u in range(HOTS):
                        one_hot(u, u)
                    group(k, 0, first=True)
                    with dve.Fori(1, GROUPS) as g:
                        group(k, g)
                    for ho in range(H):
                        add_weighted(k, GROUPS, ho)
                dve.drain().then_inc(S["complete"], 1)
                if l == 0:
                    for i in range(1, NK // 2, 2):
                        dve.wait_ge(S["back"], i + 1)
                        V.tensor_scalar(f_rows[:, 2 * i:2 * i + 2, :],
                                        bank[4 + i % 4][:P, :].rearrange("p (k d) -> p k d", k=2), 0.0, None, ALU.max)\
                            .then_inc(S["back_v"], 1)
                    dve.wait_ge(S["back"], NK // 2)
                    V.tensor_scalar(res[:, 0, 0:N], res[:, 0, 0:N], 0.0, None, ALU.max).then_inc(S["relu"], 1)
                else:
                    for i in range(NK // 2):
                        dve.wait_ge(S["back"], i + 1)
                        V.tensor_tensor(x_rows[:, 2 * i:2 * i + 2, :], x_rows[:, 2 * i:2 * i + 2, :],
                                        bank[4 + i % 4][:P, :].rearrange("p (k d) -> p k d", k=2), ALU.add)\
                            .then_inc(S["back_v"], 1)

            layer_norm(2, lambda k: dve.wait_ge(L[1]["back_v"], k // 2 + 1))

            wide = [P, NK, EXPERTS]
            dve.wait_ge(logits_done, 1)
            dve.wait_ge(gate_in, 2 * 16)
            V.tensor_tensor(lg[:, 0], bank[2][:P, 0:NK * EXPERTS].rearrange("p (k e) -> p k e", k=NK),
                            gate_b[:, None, :].to_broadcast(wide), ALU.add)
            dve.drain()
            V.tensor_reduce(tok[:, 0, :], lg[:, 0], AX.X, ALU.max)
            dve.drain()
            V.tensor_tensor(lg[:, 0], lg[:, 0], tok[:, 0, :, None].to_broadcast(wide), ALU.subtract)\
                .then_inc(scores_ready, 1)
            dve.wait_ge(exps_ready, 1)
            V.tensor_reduce(tok[:, 1, :], lg[:, 1], AX.X, ALU.add)
            dve.drain()
            V.reciprocal(tok[:, 2, :], tok[:, 1, :])
            dve.drain()
            V.tensor_tensor(lg[:, 2], lg[:, 1], tok[:, 2, :, None].to_broadcast(wide), ALU.mult)
            dve.drain()
            best = tok[:, 3, :]
            V.tensor_reduce(best, lg[:, 2], AX.X, ALU.max)
            dve.drain()
            V.tensor_tensor(lg[:, 3], lg[:, 2], tok[:, 3, :, None].to_broadcast(wide), ALU.is_equal)
            dve.drain()
            V.scalar_tensor_tensor(lg[:, 0], e_iota[:, None, :].to_broadcast(wide), float(-EXPERTS), lg[:, 3],
                                   ALU.add, ALU.mult)
            dve.drain()
            V.tensor_reduce(tok[:, 4, :], lg[:, 0], AX.X, ALU.min)
            dve.drain()
            V.tensor_scalar(tok[:, 5, :], tok[:, 4, :], 0.0, float(-EXPERTS), ALU.is_equal, ALU.mult)
            dve.drain()
            V.tensor_tensor(tok[:, 4, :], tok[:, 4, :], tok[:, 5, :], ALU.add)
            dve.drain()
            for e in range(EXPERTS):
                V.tensor_scalar(picked[:, e, :], tok[:, 4, :], float(e - EXPERTS), None, ALU.is_equal)
            dve.drain()
            for e in range(EXPERTS):
                last = V.tensor_tensor_scan(counts[:, e, :], picked[:, e, :], zeros[:P, 0:NK], 0.0, ALU.add, ALU.add)
            last.then_inc(totals_ready, 1)
            dve.wait_ge(before_ready, 1)
            place = lg[:, 1].rearrange("p k e -> p (k e)").rearrange("p (e k) -> p e k", e=EXPERTS)
            V.tensor_tensor(place, counts[:, :, :],
                            bank[3][:P, 0:EXPERTS, None].to_broadcast([P, EXPERTS, NK]), ALU.add)
            dve.drain()
            V.tensor_tensor(place, place, picked[:, :, :], ALU.mult)
            dve.drain()
            V.tensor_reduce(tok[:, 5, :], place.rearrange("p e k -> p k e"), AX.X, ALU.add)
            dve.drain()
            kept = tok[:, 6, :]
            V.tensor_scalar(kept, tok[:, 5, :], float(CAP), None, ALU.is_le)
            V.scalar_tensor_tensor(tok[:, 7, :], tok[:, 4, :], float(SLOTS), tok[:, 5, :], ALU.mult, ALU.add)
            dve.drain()
            V.tensor_scalar(tok[:, 7, :], tok[:, 7, :], float(EXPERTS * SLOTS - 1), None, ALU.add)
            V.tensor_scalar(tok[:, 9, :], kept, float(-NO_ROW), float(NO_ROW), ALU.mult, ALU.add)
            V.tensor_scalar(tok[:, 10, :], kept, float(NO_ROW), None, ALU.mult)
            dve.drain()
            V.tensor_tensor(tok[:, 9, :], tok[:, 7, :], tok[:, 9, :], ALU.add)
            dve.drain()
            V.tensor_copy(slot_to[:, :], tok[:, 9, :]).then_inc(slots_ready, 1)
            V.tensor_tensor(tok[:, 10, :], tok[:, 10, :], token_f[:, :], ALU.add)
            V.tensor_copy(token_info[:, :, 0], token_f[:, :])
            V.tensor_copy(token_info[:, :, 1].bitcast(F32), best)
            dve.drain()
            V.tensor_copy(token_over[:, :], tok[:, 10, :]).then_inc(info_ready, 1)

            dve.sem_inc(slot_cols_v, 1)
            dve.sem_inc(slot_cols_a, 1)
            dve.sem_inc(mid_v, 1)
            dve.sem_inc(mid_a, 1)

            def result(half, v):
                e = half * 2 + v
                dve.wait_ge(y_scaled, e * SLOT_TILES + SLOT_TILES)
                V.tensor_scalar(y_finite[:, :, :], y_raw[v], 0.0, 0.0, ALU.mult, ALU.is_equal)
                if not isinstance(half, int):
                    dve.wait_ge(y_sent[v], half * (SLOT_TILES * 16))
                dve.wait_ge(y_range, e + 1)
                V.tensor_tensor(y_out[v], y_over, y_under, ALU.add)
                dve.drain()
                V.copy_predicated(y_out[v], y_finite[:, :, :], y_raw[v])
                dve.drain()
                dve.wait_ge(slot_res_in[v], half * 16 + 16)
                V.tensor_tensor(y_out[v], y_out[v], slot_res[v], ALU.add).then_inc(y_result, 1)

            def expert(half, v, first):
                e = half * 2 + v
                dve.wait_ge(slots_turned, e * H + 1)
                V.tensor_copy(slot_cols[v][:, 0, :], bank[4][:, 0:SLOTS]).then_inc(slot_cols_v, 1)
                for t in range(1, FT, 2):
                    dve.wait_ge(mid_done, e * FT + (t + 1))
                    V.tensor_scalar(hmid[v][:, t, :], bank[1][:, 0:SLOTS],
                                    bias_cols[:, bass.ds(e * FT + t, 1)], 0.0, ALU.add, ALU.max).then_inc(mid_v, 1)
                if not first:
                    result(half - (1 - v), 1 - v)

            expert(0, 0, True)
            expert(0, 1, False)
            expert(1, 0, False)
            expert(1, 1, False)
            with dve.Fori(2, EXPERTS // 2) as half:
                for v in range(2):
                    expert(half, v, False)
            result(EXPERTS // 2 - 1, 1)


INPUTS = ["x", "src", "dst", "edge_type_8", "L0_gnn_W1", "L0_gnn_self_w1", "L0_gnn_b1", "L0_gnn_W2",
          "L0_gnn_self_w2", "L0_gnn_b2", "L0_ffn_gate_w", "L0_ffn_gate_b", "L0_ffn_w1", "L0_ffn_b1",
          "L0_ffn_w2", "L0_ffn_b2"]


SHAPES = {"x": (N, D), "src": (E,), "dst": (E,), "edge_type_8": (E,),
          "L0_ffn_gate_w": (D, EXPERTS), "L0_ffn_gate_b": (EXPERTS,), "L0_ffn_w1": (EXPERTS, D, FF),
          "L0_ffn_b1": (EXPERTS, FF), "L0_ffn_w2": (EXPERTS, FF, D), "L0_ffn_b2": (EXPERTS, D)}
for _l in "12":
    SHAPES |= {f"L0_gnn_W{_l}": (R, D, D), f"L0_gnn_self_w{_l}": (D, D), f"L0_gnn_b{_l}": (D,)}


def declare(nc):
    io = {n: nc.dram_tensor(f"in_{n}", SHAPES[n], I32 if n in ("src", "dst", "edge_type_8") else F32,
                            kind="ExternalInput").ap() for n in INPUTS}
    build(nc, io, nc.dram_tensor("out", (N, D), F32, kind="ExternalOutput").ap())


def kernel(**inputs):
    import concourse.bacc as bacc
    from concourse.bass_utils import run_bass_kernel_spmd

    nc = bacc.Bacc("TRN2", target_bir_lowering=False, num_devices=1)
    declare(nc)
    arrays = {f"in_{n}": np.ascontiguousarray(inputs[n]) for n in INPUTS}
    return run_bass_kernel_spmd(nc, [arrays], core_ids=[0]).results[0]["out"]
```

```python
from contextlib import ExitStack

import numpy as np
import concourse.bass as bass
from concourse import mybir

F32 = mybir.dt.float32
R32 = mybir.dt.float32r
I32 = mybir.dt.int32
U32 = mybir.dt.uint32
ALU = mybir.AluOpType
ACT = mybir.ActivationFunctionType
AX = mybir.AxisListType

N, D, R, E = 2500, 256, 8, 40000
P = 125
NK = N // P
H = D // 128
ROW = 2 * D + 2
TERMS = R + 1
CHUNKS = E // P
GROUP_CHUNKS = 20
GROUPS = CHUNKS // GROUP_CHUNKS
WIN = 14
KEYS = R * WIN
GROUP_WIN = 176
WINDOW_PASSES = -(-N // WIN)
NPAD = ((WINDOW_PASSES - 1) * WIN + GROUP_WIN + 127) // 128 * 128
EDGE_TILE, EDGE_TILES = 80, 4
RING = 20
HOTS = 10
OFFSETS = 10
SUMS = 4
STAGE = 10
STAGES = GROUP_CHUNKS // STAGE
SPAN = GROUP_WIN * R * H
EXPERTS, FF = 8, 1024
GATE_NODES = 128 // EXPERTS
GATE_AT = 128 - EXPERTS
POOL_ROWS = (3, 11, 19)
SUMMED_CREDIT = RING + 1
ADDED_CREDIT = SUMMED_CREDIT + 1
W_STEPS = R * H * H
SELF_BLOCKS = 5
SELF_COLS = N // SELF_BLOCKS
SELF_AFTER = (6, 7, 8, 9, 12, 16, 19, 19, 19, 19)
STAGE_BEFORE = (4, 6)
EPS = 1e-5

FT = FF // 128
CAP = -(-5 * N // (4 * EXPERTS))
SLOT_TILE, SLOT_TILES = 98, 4
SLOTS = SLOT_TILE * SLOT_TILES
assert STAGES == 2 and len(SELF_AFTER) == SELF_BLOCKS * H and SELF_AFTER[-1] == GROUP_CHUNKS - 1
assert RING == GROUP_CHUNKS and CAP <= SLOTS and GROUPS % 2 == 0 and RING % STAGE == 0 and GROUP_CHUNKS % RING == 0
B2_AT = EXPERTS * FT
GNN_AT = B2_AT + EXPERTS * H
BIASES = GNN_AT + 2 * H
NO_ROW = 8192
FLT_MAX = 3.4028234663852886e38
NAN_INF_TO = 10000.0


def w_steps_after(u):
    first, slots = 1, GROUP_CHUNKS - 3
    done = lambda v: min(W_STEPS, max(0, (v - first) * W_STEPS // slots))
    return range(done(u), done(u + 1))


def build(nc, io, out):
    with ExitStack() as ctx:
        def sb(name, shape, dt=F32):
            return ctx.enter_context(nc.sbuf_tensor(name, shape, dt))

        def sem(name):
            return ctx.enter_context(nc.semaphore(name))

        table = [nc.dram_tensor(f"table{l}", (N, D), F32, kind="Internal").ap() for l in range(2)]
        disp = nc.dram_tensor("dispatched", (EXPERTS * SLOTS, ROW), F32, kind="Internal").ap()

        rows = sb("rows", [P, NK, ROW])
        f_rows, x_rows = rows[:, :, 0:D], rows[:, :, D:2 * D]
        token_info = rows[:, :, 2 * D:ROW].bitcast(U32)
        edges_t = sb("edges_t", [P, 3, CHUNKS + GROUP_CHUNKS])
        spans = sb("spans", [EDGE_TILE, 2, EDGE_TILES])
        first_start = sb("first_start", [1, CHUNKS])[:, :]
        flag = sb("flag", [1, 16])
        start_row = sb("start_row", [1, CHUNKS])
        off_i = sb("off_i", [1, CHUNKS], I32)
        base_i = sb("base_i", [1, GROUPS], I32)
        passes_i = sb("passes_i", [1, 1], I32)
        key = sb("key", [P, CHUNKS + HOTS])
        key_t = sb("key_t", [P, 3, CHUNKS])
        off_f = key_t[0:1, 2, :]
        stage = sb("stage", [P, STAGES, STAGE], U32)
        ident = sb("ident", [128, 128])
        tri = sb("tri", [P, P])
        ones = sb("ones", [128, 128])
        empty_rows = sb("empty_rows", [128, 2, ROW])
        zeros = empty_rows[:, 0, 0:2 * D]
        key_iota_i = sb("key_iota_i", [P, KEYS], I32)
        key_iota = sb("key_iota", [P, KEYS])
        e_iota_i = sb("e_iota_i", [P, EXPERTS], I32)
        e_iota = sb("e_iota", [P, EXPERTS])
        bias_rows = sb("bias_rows", [BIASES, 128])
        bias_cols = sb("bias_cols", [128, BIASES])
        stats = sb("stats", [P, NK, 6])
        norms = sb("norms", [P, 2, 7, NK])
        mean, inv_std = ([norms[:, n, i, :] for n in range(2)] for i in (0, 6))
        gate_wide = sb("gate_wide", [128, H, 2 * GATE_AT + EXPERTS])
        gate_w = gate_wide[:, :, GATE_AT:GATE_AT + EXPERTS]
        gate_cols = sb("gate_cols", [128, 2, P])
        gate_b = sb("gate_b", [P, EXPERTS])
        norm_gate = sb("norm_gate", [P, NK + 1, EXPERTS])
        tok = sb("tok", [P, 12, NK])
        slot_to = sb("slot_to", [P, NK], U32)
        token_i = sb("token_i", [P, NK], I32)
        token_f = sb("token_f", [P, NK])
        token_over = sb("token_over", [P, NK], U32)
        slot_info = [sb(f"slot_info{v}", [SLOT_TILE, SLOT_TILES, 2], U32) for v in range(2)]
        w_raw = sb("w_raw", [128, FT * D * 2])

        def in_turn(stack, name, shape, dt=F32):
            return stack.enter_context(nc.sbuf_tensor(name, shape, dt))

        with ExitStack() as graph:
            ring = in_turn(graph, "ring", [P, RING, D])
            hot = in_turn(graph, "hot", [P, HOTS, KEYS])
            accum = in_turn(graph, "accum", [128, 2 * SPAN])
            weights = [in_turn(graph, f"weights{l}", [128, H, TERMS, D]) for l in range(2)]
            cols = [in_turn(graph, f"cols{i}", [128, H, NPAD]) for i in range(2)]
        ring_flat = ring[:, :, :].rearrange("p q d -> p (q d)")
        edges_i = ring_flat[:EDGE_TILE, 0:1500].bitcast(I32).rearrange("q (j t e) -> q j t e", j=3, t=EDGE_TILES)
        edges_f = ring_flat[:EDGE_TILE, 1500:3000].rearrange("q (j t e) -> q j t e", j=3, t=EDGE_TILES)
        low, spread, place_in_group = (ring_flat[0:1, 3000 + i * CHUNKS:3000 + (i + 1) * CHUNKS] for i in range(3))

        gate_parts = sb("gate_parts", [P, 2, NK, EXPERTS])
        lg = sb("lg", [P, 4, NK, EXPERTS])
        picked = sb("picked", [P, EXPERTS, NK])
        counts = sb("counts", [P, EXPERTS, NK])
        y_finite = sb("y_finite", [SLOT_TILE, SLOT_TILES, D], mybir.dt.uint8)
        w_hi, w_lo = sb("w_hi", [128, FT * D * 2], R32), sb("w_lo", [128, FT * D * 2], R32)
        slot_rows, slot_res, y_raw, y_out = (
            [sb(f"{name}{v}", [SLOT_TILE, SLOT_TILES, D])[:, :, :] for v in range(2)]
            for name in ("slot_rows", "slot_res", "y_raw", "y_out"))
        slot_hi, slot_lo = sb("slot_hi", [128, H, SLOTS], R32), sb("slot_lo", [128, H, SLOTS], R32)
        y_cols = sb("y_cols", [128, H, SLOTS])
        y_over, y_under = (sb(name, [SLOT_TILE, SLOT_TILES, D])[:, :, :] for name in ("y_over", "y_under"))
        mid_hi = sb("mid_hi", [128, FT, SLOTS], R32)
        with nc.sbuf_tensor("mid_full", [128, FT, SLOTS], F32) as mid_full:
            pass
        mid_lo = sb("mid_lo", [128, FT, SLOTS], R32)

        def first_weights(w):
            return w[:, 0:2048].rearrange("p (h f) -> p h f", h=H)

        def second_weights(w):
            return w[:, 2048:4096].rearrange("p (t d) -> p t d", t=FT)

        bank = [ctx.enter_context(nc.psum_tensor(f"bank{i}", [128, 512], F32)) for i in range(8)]
        chunk_sum = [bank[4 + i][:, 0:H * KEYS].rearrange("p (h k) -> p h k", h=H) for i in range(SUMS)]

        edges_in, gate_in, bias_in = sem("edges_in"), sem("gate_in"), sem("bias_in")
        x_in = [sem(f"x_in{i}") for i in range(4)]
        weights_in = [sem("weights_in0"), sem("weights_in1")]
        consts = sem("consts")
        edges_as_f, spans_done = sem("edges_as_f"), sem("spans_done")
        edges_turned, spans_turned = sem("edges_turned"), sem("spans_turned")
        edges_copied = sem("edges_copied")
        bias_turned, bias_copied = sem("bias_turned"), sem("bias_copied")
        var_ready, std_ready = sem("var_ready"), sem("std_ready")
        rows_ready = sem("rows_ready")
        rows_ready_p = sem("rows_ready_p")
        norm_ready = sem("norm_ready")
        turned, turned_used = sem("turned"), sem("turned_used")
        passes_ready = sem("passes_ready")
        disp_empty, disp_in, over_out = sem("disp_empty"), sem("disp_in"), sem("over_out")
        L = []
        for l in range(2):
            s = lambda name: sem(f"{name}_{l}")
            L.append(dict(
                table_in=s("table_in"), starts=s("starts"), starts_wide=s("starts_wide"),
                staged=s("staged"), slot=[s(f"slot{q}") for q in range(RING)],
                hot=s("hot"), summed=s("summed"), added=s("added"), zeroed=s("zeroed"), w_done=s("w_done"),
                w_added=s("w_added"), self_done=s("self_done"), self_out=s("self_out"),
                complete=s("complete"), relu=s("relu"), back=s("back"), back_a=s("back_a"), back_v=s("back_v"),
                claimed=s("claimed")))
        gate_products, gate_cols_out, gate_turned, norm_gate_out = (
            sem("gate_products"), sem("gate_cols_out"), sem("gate_turned"), sem("norm_gate_out"))
        scores_ready, exps_ready = sem("scores_ready"), sem("exps_ready")
        totals_ready, before_ready = sem("totals_ready"), sem("before_ready")
        slots_ready = sem("slots_ready")
        pair = lambda name: [sem(f"{name}0"), sem(f"{name}1")]
        w1_in, w2_in = sem("w1_in"), sem("w2_in")
        slot_rows_in, slot_res_in, info_in = map(pair, ("slot_rows_in", "slot_res_in", "info_in"))
        w1_hi, w1_split, w2_hi, w2_split = sem("w1_hi"), sem("w1_split"), sem("w2_hi"), sem("w2_split")
        slots_turned, slots_hi, slots_split = sem("slots_turned"), sem("slots_hi"), sem("slots_split")
        mid_done, mid_out, mid_split = sem("mid_done"), sem("mid_out"), sem("mid_split")
        y_done, y_cols_in = sem("y_done"), sem("y_cols_in")
        y_turned, y_scaled, y_result, y_sent = sem("y_turned"), sem("y_scaled"), sem("y_result"), pair("y_sent")

        def in_register(eng, value):
            return value if isinstance(value, int) else eng.snap(value)

        def passes_of(eng):
            eng.wait_ge(passes_ready, 1)
            return eng.value_load(passes_i[0:1, 0:1], min_val=1, max_val=WINDOW_PASSES)

        def strided_cols(buf, h, k0, nk):
            return buf[:, h, 0:N].rearrange("c (p k) -> c k p", k=NK)[:, k0:k0 + nk, :]

        def rows_normalised(eng, before, k):
            by_pool = sum(row < k for row in POOL_ROWS)
            eng.wait_ge(rows_ready, before * (NK - len(POOL_ROWS)) + k - by_pool)
            if by_pool + before:
                eng.wait_ge(rows_ready_p, before * len(POOL_ROWS) + by_pool)

        block = ctx.enter_context(nc.Block())

        @block.sync
        def _(sp):
            x_v = io["x"].rearrange("(p k) d -> p k d", k=NK)
            for i in range(4):
                sp.dma_start(x_rows[:, 5 * i:5 * i + 5, :], x_v[:, 5 * i:5 * i + 5, :]).then_inc(x_in[i], 16)
            sp.dma_start(bias_rows[0:B2_AT, :], io["L0_ffn_b1"].rearrange("e (t c) -> (e t) c", c=128))\
              .then_inc(bias_in, 16)
            sp.dma_start(bias_rows[B2_AT:GNN_AT, :], io["L0_ffn_b2"].rearrange("e (h c) -> (e h) c", c=128))\
              .then_inc(bias_in, 16)
            for l in range(2):
                at = GNN_AT + H * l
                sp.dma_start(bias_rows[at:at + H, :], io[f"L0_gnn_b{l + 1}"].rearrange("(h c) -> h c", c=128))\
                  .then_inc(bias_in, 16)

            def load_weights(l, h):
                sp.dma_start(weights[l][:, h, 0:R, :],
                             io[f"L0_gnn_W{l + 1}"][:, h * 128:h * 128 + 128, :].rearrange("r c o -> c r o"))\
                  .then_inc(weights_in[l], 16)
                sp.dma_start(weights[l][:, h, R, :], io[f"L0_gnn_self_w{l + 1}"][h * 128:h * 128 + 128, :])\
                  .then_inc(weights_in[l], 16)

            for h in range(H):
                load_weights(0, h)
            t_v = table[0].rearrange("(p k) d -> p k d", k=NK)
            for i in range(5):
                rows_normalised(sp, 0, 4 * i + 4)
                sp.dma_start(t_v[:, 4 * i:4 * i + 4, :], f_rows[:, 4 * i:4 * i + 4, :]).then_inc(L[0]["table_in"], 16)
            sp.wait_ge(consts, 1)
            for i in range(EXPERTS):
                sp.wait_ge(L[0]["w_done"], 2 * H + (2 * i + 1) * H)
                if i < H:
                    load_weights(1, i)
                for j in range(0, SLOT_TILES, 2):
                    sp.wait_ge(L[0]["w_done"], 2 * H + (2 * i + 1 + j // 2) * H)
                    sp.dma_start(disp[i * SLOTS:(i + 1) * SLOTS, :].rearrange("(p j) d -> p j d", j=SLOT_TILES)
                                 [:, j:j + 2, :], empty_rows[0:SLOT_TILE, :, :])\
                      .then_inc(disp_empty, 16)
            sp.dma_start(gate_w, io["L0_ffn_gate_w"].rearrange("(h c) e -> c h e", c=128)).then_inc(gate_in, 16)
            sp.dma_start(gate_b[:, :], io["L0_ffn_gate_b"].rearrange("(a e) -> a e", a=1).to_broadcast([P, EXPERTS]))\
              .then_inc(gate_in, 16)
            t_v = table[1].rearrange("(p k) d -> p k d", k=NK)
            for i in range(5):
                sp.wait_ge(L[0]["back_a"], i + 1)
                sp.wait_ge(L[0]["back_v"], i + 1)
                sp.dma_start(t_v[:, 4 * i:4 * i + 4, :], f_rows[:, 4 * i:4 * i + 4, :]).then_inc(L[1]["table_in"], 16)

            def load_w1(e):
                sp.dma_start(w_raw[:, 0:2048], io["L0_ffn_w1"][bass.ds(e, 1), :, :]
                             .rearrange("a (h c) f -> c (a h) f", c=128)).then_inc(w1_in, 16)

            def load_w2(e):
                sp.dma_start(w_raw[:, 2048:4096], io["L0_ffn_w2"][bass.ds(e, 1), :, :]
                             .rearrange("a (t c) d -> c (a t) d", c=128)).then_inc(w2_in, 16)

            def slot_part(e, first, last):
                return disp[bass.ds(e * SLOTS, SLOTS), first:last].rearrange("(p j) d -> p j d", j=SLOT_TILES)

            def load_ahead(e, v, more=True):
                if more:
                    sp.wait_ge(w1_split, e)
                    load_w1(e)
                    if not (isinstance(e, int) and e < 2):
                        sp.wait_ge(slots_turned, (e - 1) * H)
                    sp.dma_start(slot_rows[v], slot_part(e, 0, D)).then_inc(slot_rows_in[v], 16)
                    sp.wait_ge(w2_split, e * 4)
                    load_w2(e)
                if not (isinstance(e, int) and e < 3):
                    sp.wait_ge(y_result, e - 2)
                sp.dma_start(slot_res[1 - v], slot_part(e - 1, D, 2 * D)).then_inc(slot_res_in[1 - v], 16)
                if not (isinstance(e, int) and e < 3):
                    sp.wait_ge(y_sent[1 - v], (e + v - 2) * (SLOT_TILES * 8))
                sp.dma_start(slot_info[1 - v][:, :, :], slot_part(e - 1, 2 * D, ROW).bitcast(U32))\
                  .then_inc(info_in[1 - v], 16)
            load_w1(0)
            load_w2(0)
            sp.wait_ge(disp_in, NK * 16)
            sp.dma_start(slot_rows[0], slot_part(0, 0, D)).then_inc(slot_rows_in[0], 16)
            load_ahead(1, 1)
            load_ahead(2, 0)
            with sp.Fori(1, EXPERTS // 2 - 1) as half:
                load_ahead(half * 2 + 1, 1)
                load_ahead(half * 2 + 2, 0)
            load_ahead(EXPERTS - 1, 1)
            load_ahead(EXPERTS, 0, more=False)

        @block.gpsimd
        def _(pool):
            pool.memset(empty_rows[:, :, :], 0.0)
            pool.memset(ident[:, :], 0.0)
            pool.memset(gate_wide[:, :, :], 0.0)
            pool.memset(tri[:, :], 1.0)
            pool.memset(ones[:, :], 1.0)
            pool.iota(token_i[:, :], pattern=[[1, NK]], base=0, channel_multiplier=NK)
            pool.iota(key_iota_i[:, :], pattern=[[1, KEYS]], base=0, channel_multiplier=0)
            pool.iota(e_iota_i[:, :], pattern=[[1, EXPERTS]], base=0, channel_multiplier=0)
            pool.drain()
            pool.affine_select(out=ident[:, :], in_=ident[:, :], compare_op=ALU.not_equal, fill=1.0, base=0,
                               pattern=[[-1, 128]], channel_multiplier=1)
            pool.memset(empty_rows[:, :, 2 * D:2 * D + 1].bitcast(U32), NO_ROW)
            pool.affine_select(out=tri[:, :], in_=tri[:, :], compare_op=ALU.is_gt, fill=0.0, base=0,
                               pattern=[[1, P]], channel_multiplier=-1)
            pool.tensor_copy(key_iota[:, :], key_iota_i[:, :])
            pool.tensor_copy(e_iota[:, :], e_iota_i[:, :])
            pool.tensor_copy(token_f[:, :], token_i[:, :])
            pool.drain().then_inc(consts, 1)

            def normalise(nth):
                pool.wait_ge(norm_ready, nth)
                for k in POOL_ROWS:
                    pool.tensor_scalar(f_rows[:, k, :], x_rows[:, k, :], mean[nth - 1][:, k:k + 1],
                                       inv_std[nth - 1][:, k:k + 1],
                                       ALU.subtract, ALU.mult).then_inc(rows_ready_p, 1)

            normalise(1)

            for l in range(2):
                S = L[l]
                passes = passes_of(pool)
                with pool.Fori(0, passes) as k:
                    with pool.Fori(0, GROUPS) as g:
                        for u in range(GROUP_CHUNKS):
                            q = u % RING
                            if u % STAGE == 0:
                                pool.wait_ge(S["staged"], k * (GROUPS * STAGES) + g * STAGES + (u // STAGE + 1))
                                pool.wait_ge(S["summed"],
                                             k * CHUNKS + g * GROUP_CHUNKS + (u + STAGE + SUMMED_CREDIT - RING))
                                pool.sem_inc(S["claimed"], 1)
                                pool.wait_ge(S["table_in"], 5 * 16)
                            pool.indirect_dma_start(
                                ring[:, q, :], None, table[l],
                                bass.IndirectOffsetOnAxis(ap=stage[:, u // STAGE, u % STAGE:u % STAGE + 1], axis=0),
                            ).then_inc(S["slot"][q], 16)

            normalise(2)

            pool.wait_ge(disp_empty, 2 * EXPERTS * 16)
            pool.wait_ge(slots_ready, 1)
            for k in range(NK):
                if k % 5 == 0:
                    rows_normalised(pool, 1, k + 5)
                pool.indirect_dma_start(
                    disp, bass.IndirectOffsetOnAxis(ap=slot_to[:, k:k + 1], axis=0), rows[:, k, :], None,
                    bounds_check=EXPERTS * SLOTS - 1, oob_is_err=False).then_inc(disp_in, 16)
            for k in range(NK):
                pool.indirect_dma_start(
                    out, bass.IndirectOffsetOnAxis(ap=token_over[:, k:k + 1], axis=0), x_rows[:, k, :], None,
                    bounds_check=N - 1, oob_is_err=False).then_inc(over_out, 16)

            def send(half, v, part=None):
                e = half * 2 + v
                pool.wait_ge(y_result, e + 1 + (part or 0))
                pool.sem_inc(L[1]["claimed"], 1)
                for j in range(SLOT_TILES) if part is None else range(2 * part, 2 * part + 2):
                    pool.indirect_dma_start(
                        out, bass.IndirectOffsetOnAxis(ap=slot_info[v][:, j, 0:1], axis=0), y_out[v][:, j, :], None,
                        bounds_check=N - 1, oob_is_err=False).then_inc(y_sent[v], 16)

            with pool.Fori(0, EXPERTS // 2 - 1) as half:
                for v in range(2):
                    send(half, v)
            send(EXPERTS // 2 - 1, 0)
            for part in range(2):
                send(EXPERTS // 2 - 1, 1, part)
            pool.wait_ge(over_out, NK * 16)
            for v in range(2):
                pool.wait_ge(y_sent[v], EXPERTS // 2 * SLOT_TILES * 16)

        @block.scalar
        def _(act):
            for j, name in enumerate(("dst", "edge_type_8", "src")):
                act.dma_start(edges_i[:, j, :, :],
                              io[name].rearrange("(t q e) -> q t e", q=EDGE_TILE, e=P)).then_inc(edges_in, 16)
            act.wait_ge(edges_in, 3 * 16)
            for j in range(3):
                nc.scalar.activation(edges_f[:, j], edges_i[:, j], ACT.Copy).then_inc(edges_as_f, 1)
            act.wait_ge(var_ready, 1)
            nc.scalar.activation(norms[:, 0, 3, :], norms[:, 0, 2, :], ACT.Sqrt).then_inc(std_ready, 1)
            act.wait_ge(edges_turned, 3)
            nc.scalar.activation(edges_t[:, 0, 0:CHUNKS], bank[4][:P, 0:CHUNKS], ACT.Copy).then_inc(edges_copied, 1)
            nc.scalar.activation(edges_t[:, 1, 0:CHUNKS], bank[5][:P, 0:CHUNKS], ACT.Copy, scale=float(WIN), bias=1.0)\
                .then_inc(edges_copied, 1)
            nc.scalar.activation(edges_t[:, 2, CHUNKS:], bank[6][:P, 0:GROUP_CHUNKS], ACT.Copy)
            nc.scalar.activation(edges_t[:, 2, 0:CHUNKS], bank[6][:P, 0:CHUNKS], ACT.Copy).then_inc(edges_copied, 1)
            act.drain()

            def stage_indices(l, c, s):
                nc.scalar.activation(stage[:, s, :], edges_t[:, 2, bass.ds(c, STAGE)], ACT.Copy)\
                    .then_inc(L[l]["staged"], 1)

            def clear_accum(l, odd):
                nc.scalar.activation(
                    accum[:, bass.ds(odd * SPAN, SPAN)].rearrange("c (a b) -> c a b", b=GROUP_WIN),
                    zeros[:, None, 0:GROUP_WIN].to_broadcast([128, R * H, GROUP_WIN]), ACT.Copy)\
                    .then_inc(L[l]["zeroed"], 1)

            for s in range(STAGES):
                stage_indices(0, s * STAGE, s)
            act.wait_ge(consts, 1)
            clear_accum(0, 0)
            act.wait_ge(bias_turned, 1)
            nc.scalar.activation(bias_cols[:, :], bank[3][:, 0:BIASES], ACT.Copy)\
                .then_inc(bias_copied, 1)

            def gate_cols_copy(nth):
                act.wait_ge(gate_products, nth)
                nc.scalar.activation(gate_cols[:, :, :], bank[2][:, 0:2 * P].rearrange("c (a p) -> c a p", a=2),
                                     ACT.Copy).then_inc(gate_cols_out, 1)

            for i in range(5 * H):
                act.wait_ge(turned, i + 1)
                nc.scalar.activation(strided_cols(cols[0], i % H, 4 * (i // H), 4), bank[4 + i % 4][:, 0:4 * P]
                                     .rearrange("c (k p) -> c k p", k=4), ACT.Copy).then_inc(turned_used, 1)

            for l in range(2):
                S = L[l]

                def stage_ahead(k, g, s):
                    act.wait_ge(S["slot"][(s + 1) * STAGE - 1], k * (GROUPS * 16) + g * 16 + 16)
                    stage_indices(l, g * GROUP_CHUNKS + (GROUP_CHUNKS + s * STAGE), s)

                def ahead(k, g):
                    for s in range(STAGES):
                        stage_ahead(k, g, s)
                    act.wait_ge(S["w_done"], k * (GROUPS * H) + g * H + 2 * H)
                    clear_accum(l, (g + 1) % 2)

                if l == 1:
                    gate_cols_copy(1)
                    act.wait_ge(gate_turned, 1)
                    nc.scalar.activation(norm_gate[:, :, :], bank[3][:P, 0:(NK + 1) * EXPERTS]
                                         .rearrange("p (k e) -> p k e", e=EXPERTS), ACT.Copy).then_inc(norm_gate_out, 1)
                act.wait_ge(bias_copied, 1)
                at = GNN_AT + H * l
                for i in range(SELF_BLOCKS * H):
                    b, h = i // H, i % H
                    for s in range(STAGES):
                        if i == STAGE_BEFORE[s]:
                            stage_ahead(0, 0, s)
                    act.wait_ge(S["self_done"], i + 1)
                    nc.scalar.activation(cols[1 - l][:, h, b * SELF_COLS:(b + 1) * SELF_COLS],
                                         bank[2 + i % 2][:, 0:SELF_COLS], ACT.Identity,
                                         bias=bias_cols[:, at + h:at + h + 1]).then_inc(S["self_out"], 1)
                act.wait_ge(S["w_done"], 2 * H)
                clear_accum(l, 1)
                passes = passes_of(act)
                with act.Fori(1, GROUPS) as g:
                    ahead(0, g)
                with act.If(passes > 1):
                    with act.Fori(1, passes) as k:
                        with act.Fori(0, GROUPS) as g:
                            ahead(k, g)
                if l == 0:
                    for i in range(0, NK // 2, 2):
                        act.wait_ge(S["back"], i + 1)
                        nc.scalar.activation(f_rows[:, 2 * i:2 * i + 2, :],
                                             bank[4 + i % 4][:P, :].rearrange("p (k d) -> p k d", k=2), ACT.Relu)\
                            .then_inc(S["back_a"], 1)
                    for s in range(STAGES):
                        stage_indices(1, s * STAGE, s)
                    clear_accum(1, 0)
                    act.wait_ge(S["back"], NK // 2)
                    nc.scalar.activation(cols[1][:, 1, 0:N], cols[1][:, 1, 0:N], ACT.Relu).then_inc(S["relu"], 1)


            def split_w1(e):
                act.wait_ge(w1_in, e * 16 + 16)
                nc.scalar.activation(w_hi[:, 0:2048], w_raw[:, 0:2048], ACT.Copy).then_inc(w1_hi, 1)

            act.wait_ge(L[1]["complete"], 1)
            split_w1(0)
            act.wait_ge(var_ready, 2)
            nc.scalar.activation(norms[:, 1, 3, :], norms[:, 1, 2, :], ACT.Sqrt).then_inc(std_ready, 1)
            gate_cols_copy(2)
            act.wait_ge(scores_ready, 1)
            nc.scalar.activation(lg[:, 1], lg[:, 0], ACT.Exp).then_inc(exps_ready, 1)

            def slots_high(e):
                for h in range(H):
                    act.wait_ge(slots_turned, e * H + (h + 1))
                    nc.scalar.activation(slot_hi[:, h, :], bank[4 + h][:, 0:SLOTS], ACT.Copy).then_inc(slots_hi, 1)

            def expert(half, v, first=False, last=False):
                e = half * 2 + v
                for t in range(FT):
                    act.wait_ge(mid_done, e * FT + (t + 1))
                    nc.scalar.activation(mid_full[:, t, :], bank[t % 2][:, 0:SLOTS], ACT.Relu,
                                         bias=bias_cols[:, bass.ds(e * FT + t, 1)]).then_inc(mid_out, 1)
                    if t % 2:
                        if t == 1:
                            act.wait_ge(w2_in, e * 16 + 16)
                        at = 2048 + t // 2 * 512
                        nc.scalar.activation(w_hi[:, at:at + 512], w_raw[:, at:at + 512], ACT.Copy).then_inc(w2_hi, 1)
                if not last:
                    split_w1(e + 1)
                if not first:
                    scale(half - (1 - v), 1 - v)
                if not last:
                    slots_high(e + 1)
                for h in range(H):
                    act.wait_ge(y_done, e * H + (h + 1))
                    nc.scalar.activation(y_cols[:, h, :], bank[6 + h][:, 0:SLOTS], ACT.Identity,
                                         bias=bias_cols[:, bass.ds(B2_AT + e * H + h, 1)]).then_inc(y_cols_in, 1)

            def scale(half, v):
                e = half * 2 + v
                act.wait_ge(info_in[v], half * 16 + 16)
                for j in range(SLOT_TILES):
                    act.wait_ge(y_turned, e * 2 + (j // 2 + 1))
                    nc.scalar.activation(y_raw[v][:, j, :], bank[2 + j // 2][:SLOT_TILE, j % 2 * D:(j % 2 + 1) * D],
                                         ACT.Copy, scale=slot_info[v][:, j, 1:2].bitcast(F32)).then_inc(y_scaled, 1)

            slots_high(0)
            expert(0, 0, first=True)
            expert(0, 1)
            with act.Fori(1, EXPERTS // 2 - 1) as half:
                for v in range(2):
                    expert(half, v)
            expert(EXPERTS // 2 - 1, 0)
            expert(EXPERTS // 2 - 1, 1, last=True)
            scale(EXPERTS // 2 - 1, 1)

        @block.tensor
        def _(pe):
            pe.wait_ge(consts, 1)
            for j in range(3):
                pe.wait_ge(edges_as_f, j + 1)
                for t in range(EDGE_TILES):
                    last = nc.tensor.transpose(bank[4 + j][:P, t * EDGE_TILE:(t + 1) * EDGE_TILE], edges_f[:, j, t, :],
                                               ident[0:EDGE_TILE, 0:EDGE_TILE])
                last.then_inc(edges_turned, 1)
            pe.wait_ge(spans_done, 1)
            for m in range(2):
                for t in range(EDGE_TILES):
                    last = nc.tensor.matmul(bank[m][0:1, t * EDGE_TILE:(t + 1) * EDGE_TILE], spans[:, m, t:t + 1],
                                            ident[0:EDGE_TILE, 0:EDGE_TILE], start=True, stop=True)
            last.then_inc(spans_turned, 1)
            pe.wait_ge(bias_in, 4 * 16)
            nc.tensor.transpose(bank[3][:, 0:BIASES], bias_rows[:, :], ident[0:BIASES, 0:BIASES])\
                .then_inc(bias_turned, 1)

            def turn_rows():
                for i in range(5 * H):
                    k0, h = 4 * (i // H), i % H
                    rows_normalised(pe, 0, k0 + 4)
                    if i >= 4:
                        pe.wait_ge(turned_used, i - 3)
                    for j in range(4):
                        last = nc.tensor.transpose(bank[4 + i % 4][:, j * P:(j + 1) * P],
                                                   f_rows[:, k0 + j, h * 128:(h + 1) * 128], ident[0:P, 0:P])
                    last.then_inc(turned, 1)

            def gate_product(columns):
                pe.wait_ge(gate_in, 2 * 16)
                for part, nodes in enumerate((range(GATE_NODES), range(GATE_NODES, NK + 1))):
                    for j, k in enumerate(nodes):
                        for h in range(H):
                            at = GATE_AT - EXPERTS * j
                            what = strided_cols(columns, h, k, 1)[:, 0, :] if k < NK else ones[:, 0:P]
                            last = nc.tensor.matmul(bank[2][:, part * P:(part + 1) * P], gate_wide[:, h, at:at + 128],
                                                    what, start=(j == h == 0), stop=(k == nodes[-1] and h == H - 1))
                last.then_inc(gate_products, 1)

            def gate_turn(nth):
                pe.wait_ge(gate_cols_out, nth)
                rest = (NK + 1 - GATE_NODES) * EXPERTS
                nc.tensor.transpose(bank[3][:P, 0:128], gate_cols[:, 0, :], ident[:, :])
                nc.tensor.transpose(bank[3][:P, 128:128 + rest], gate_cols[0:rest, 1, :], ident[0:rest, 0:rest])\
                    .then_inc(gate_turned, 1)

            pe.wait_ge(edges_copied, 3)
            turn_rows()

            for l in range(2):
                S = L[l]
                pe.sem_inc(S["summed"], SUMMED_CREDIT)
                pe.sem_inc(S["w_done"], 2 * H)
                feats = cols[l]
                if l == 0:
                    pe.wait_ge(turned_used, 5 * H)
                else:
                    pe.wait_ge(L[0]["back_a"], 5)
                    pe.wait_ge(L[0]["back_v"], 5)

                def self_step(i):
                    b, ho = i // H, i % H
                    if i >= 2:
                        pe.wait_ge(S["self_out"], i - 1)
                    for h in range(H):
                        last = nc.tensor.matmul(bank[2 + i % 2][:, 0:SELF_COLS],
                                                weights[l][:, h, R, ho * 128:(ho + 1) * 128],
                                                feats[:, h, b * SELF_COLS:(b + 1) * SELF_COLS],
                                                start=(h == 0), stop=(h == H - 1))
                    last.then_inc(S["self_done"], 1)

                def weight_step(k, g, w):
                    ho, r, h = w // (R * H), w % (R * H) // H, w % H
                    if w == 0:
                        pe.wait_ge(S["added"], k * CHUNKS + g * GROUP_CHUNKS + ADDED_CREDIT)
                    if r == h == 0:
                        pe.wait_ge(S["w_added"], k * (GROUPS * H) + (g - 1) * H + (ho + 1))
                    at = ((g - 1) % 2) * SPAN + (h * R + r) * GROUP_WIN
                    ins = nc.tensor.matmul(bank[2 + ho][:, 0:GROUP_WIN], weights[l][:, h, r, ho * 128:(ho + 1) * 128],
                                           accum[:, bass.ds(at, GROUP_WIN)],
                                           start=(r == h == 0), stop=(w % (R * H) == R * H - 1))
                    if w % (R * H) == R * H - 1:
                        ins.then_inc(S["w_done"], 1)

                def group(k, g, between=lambda u: None):
                    chunks = in_register(pe, k * CHUNKS + g * GROUP_CHUNKS)
                    hots = in_register(pe, k * (CHUNKS + HOTS) + g * GROUP_CHUNKS)
                    gathers = in_register(pe, k * (GROUPS * 16) + g * 16)
                    for u in range(GROUP_CHUNKS):
                        q = u % RING
                        pe.wait_ge(S["slot"][q], gathers + 16)
                        pe.wait_ge(S["hot"], hots + (u + 1))
                        pe.wait_ge(S["added"], chunks + (u + ADDED_CREDIT - SUMS + 1))
                        for h in range(H):
                            last = nc.tensor.matmul(chunk_sum[u % SUMS][:, h, :], ring[:, q, h * 128:(h + 1) * 128],
                                                    hot[:, u % HOTS, :], start=True, stop=True)
                        last.then_inc(S["summed"], 1)
                        between(u)

                def self_steps(u):
                    if u == SELF_AFTER[0]:
                        pe.wait_ge(weights_in[l], 2 * H * 16)
                        if l == 1:
                            pe.wait_ge(L[0]["relu"], 2)
                            pe.wait_ge(norm_gate_out, 1)
                    if l == 1 and u == SUMS - 1:
                        gate_turn(1)
                    for i in range(SELF_BLOCKS * H):
                        if SELF_AFTER[i] == u:
                            self_step(i)

                def one_pass(k, between=lambda u: None):
                    pe.wait_ge(S["starts"], k + 1)
                    nc.tensor.matmul(bank[0][:P, 0:CHUNKS], ones[0:1, 0:P], start_row[0:1, :], start=True, stop=True)\
                        .then_inc(S["starts_wide"], 1)
                    if l == 1 and isinstance(k, int):
                        gate_product(cols[0])
                    group(k, 0, between)
                    if isinstance(k, int):
                        pe.wait_ge(S["self_out"], SELF_BLOCKS * H)
                    with pe.Fori(1, GROUPS) as g:
                        def weight_steps(u):
                            for w in w_steps_after(u):
                                weight_step(k, g, w)

                        group(k, g, weight_steps)
                    for w in range(W_STEPS):
                        weight_step(k, GROUPS, w)

                passes = passes_of(pe)
                one_pass(0, self_steps)
                with pe.If(passes > 1):
                    with pe.Fori(1, passes) as k:
                        one_pass(k)

                res = cols[1 - l]
                pe.wait_ge(S["complete"], 1)
                for i in range(NK // 2):
                    if i >= 4:
                        if l == 0 and i % 2 == 0:
                            pe.wait_ge(S["back_a"], (i - 4) // 2 + 1)
                        elif l == 0:
                            pe.wait_ge(S["back_v"], (i - 4) // 2 + 1)
                        else:
                            pe.wait_ge(S["back_v"], i - 3)
                    for j in range(4):
                        k0, h = 2 * i + j // H, j % H
                        last = nc.tensor.transpose(bank[4 + i % 4][:P, j * 128:(j + 1) * 128],
                                                   strided_cols(res, h, k0, 1)[:, 0, :], ident[:, :])
                    last.then_inc(S["back"], 1)

            gate_product(cols[0])
            gate_turn(2)
            pe.wait_ge(totals_ready, 1)
            nc.tensor.matmul(bank[3][:P, 0:EXPERTS], tri[:, :], counts[:, :, NK - 1], start=True, stop=True)\
                .then_inc(before_ready, 1)

            def products(to, hi, lo, x_hi, x_lo, first, last):
                nc.tensor.matmul(to, hi, x_hi, start=first, stop=False)
                nc.tensor.matmul(to, hi, x_lo, start=False, stop=False)
                return nc.tensor.matmul(to, lo, x_hi, start=False, stop=last)

            def turn_slots(half, v):
                pe.wait_ge(slot_rows_in[v], half * 16 + 16)
                for h in range(H):
                    for j in range(SLOT_TILES):
                        last = nc.tensor.transpose(bank[4 + h][:, j * SLOT_TILE:(j + 1) * SLOT_TILE],
                                                   slot_rows[v][:, j, h * 128:(h + 1) * 128],
                                                   ident[0:SLOT_TILE, 0:SLOT_TILE])
                    last.then_inc(slots_turned, 1)

            def turn_back(half, v):
                e = half * 2 + v
                pe.wait_ge(y_cols_in, e * H + H)
                if not (isinstance(e, int) and e == 0):
                    pe.wait_ge(y_scaled, e * SLOT_TILES)
                for j in range(SLOT_TILES):
                    for h in range(H):
                        at = j % 2 * D + h * 128
                        last = nc.tensor.transpose(bank[2 + j // 2][:SLOT_TILE, at:at + 128],
                                                   y_cols[:, h, j * SLOT_TILE:(j + 1) * SLOT_TILE], ident[:, :])
                    if j % 2:
                        last.then_inc(y_turned, 1)

            def expert(half, v, first=False, last_one=False):
                e = half * 2 + v
                pe.wait_ge(slots_split, e * H + H)
                pe.wait_ge(w1_split, e + 1)
                for t in range(FT):
                    if not first or t >= 2:
                        pe.wait_ge(mid_out, e * FT + (t - 1))
                    at = slice(t * 128, (t + 1) * 128)
                    for h in range(H):
                        last = products(bank[t % 2][:, 0:SLOTS],
                                        first_weights(w_hi)[:, h, at], first_weights(w_lo)[:, h, at],
                                        slot_hi[:, h, :], slot_lo[:, h, :], h == 0, h == H - 1)
                    last.then_inc(mid_done, 1)
                if not first:
                    turn_back(half - (1 - v), 1 - v)
                if not last_one:
                    turn_slots(half + v, 1 - v)
                for ho in range(H):
                    if not first:
                        pe.wait_ge(y_cols_in, e * H)
                    at = slice(ho * 128, (ho + 1) * 128)
                    for t in range(FT):
                        if ho == 0 and t % 2 == 0:
                            pe.wait_ge(mid_split, e * (FT // 2) + (t // 2 + 1))
                            pe.wait_ge(w2_split, e * (FT // 2) + (t // 2 + 1))
                        last = products(bank[6 + ho][:, 0:SLOTS],
                                        second_weights(w_hi)[:, t, at], second_weights(w_lo)[:, t, at],
                                        mid_hi[:, t, :], mid_lo[:, t, :], t == 0, t == FT - 1)
                    last.then_inc(y_done, 1)

            turn_slots(0, 0)
            expert(0, 0, first=True)
            expert(0, 1)
            with pe.Fori(1, EXPERTS // 2 - 1) as half:
                for v in range(2):
                    expert(half, v)
            expert(EXPERTS // 2 - 1, 0)
            expert(EXPERTS // 2 - 1, 1, last_one=True)
            turn_back(EXPERTS // 2 - 1, 1)

        @block.vector
        def _(dve):
            V = nc.vector
            off_regs = [dve.alloc_register(f"off{i}") for i in range(OFFSETS)]
            V.memset(key[:, CHUNKS:], -1.0)
            for i in range(2):
                V.memset(cols[i][:, :, N:NPAD], 0.0)

            def x_arrived(k):
                dve.wait_ge(x_in[k // 5], 16)
                if k == 15:
                    dve.wait_ge(edges_as_f, 1)
                    V.tensor_reduce(spans[:, 0, :], edges_f[:, 0], AX.X, ALU.min)
                    V.tensor_reduce(spans[:, 1, :], edges_f[:, 0], AX.X, ALU.max).then_inc(spans_done, 1)

            def layer_norm(nth, arrived):
                ln = norms[:, nth - 1]
                for k in range(NK):
                    arrived(k)
                    V.bn_stats(stats[:, k, :], x_rows[:, k, :])
                dve.drain()
                V.tensor_tensor(ln[:, 0, :], stats[:, :, 1], stats[:, :, 4], ALU.add)
                V.tensor_tensor(ln[:, 1, :], stats[:, :, 1], stats[:, :, 4], ALU.subtract)
                V.tensor_tensor(ln[:, 2, :], stats[:, :, 2], stats[:, :, 5], ALU.add)
                dve.drain()
                V.tensor_scalar(ln[:, 0, :], ln[:, 0, :], 0.5, None, ALU.mult)
                V.scalar_tensor_tensor(ln[:, 5, :], ln[:, 1, :], 0.25, ln[:, 1, :], ALU.mult, ALU.mult)
                V.tensor_scalar(ln[:, 2, :], ln[:, 2, :], 1.0 / D, EPS, ALU.mult, ALU.add)
                dve.drain()
                V.tensor_tensor(ln[:, 2, :], ln[:, 2, :], ln[:, 5, :], ALU.add).then_inc(var_ready, 1)
                dve.wait_ge(std_ready, nth)
                V.reciprocal(ln[:, 4, :], ln[:, 3, :])
                dve.drain()
                V.tensor_tensor(ln[:, 4, :], ln[:, 4, :], ln[:, 2, :], ALU.mult)
                dve.drain()
                V.tensor_tensor(ln[:, 4, :], ln[:, 4, :], ln[:, 3, :], ALU.add)
                dve.drain()
                V.tensor_scalar(ln[:, 4, :], ln[:, 4, :], 0.5, None, ALU.mult)
                dve.drain()
                V.reciprocal(ln[:, 6, :], ln[:, 4, :])
                dve.drain().then_inc(norm_ready, 1)

            def normalise(nth, first, last):
                for k in range(first, last):
                    if k not in POOL_ROWS:
                        V.tensor_scalar(f_rows[:, k, :], x_rows[:, k, :], mean[nth - 1][:, k:k + 1],
                                        inv_std[nth - 1][:, k:k + 1], ALU.subtract, ALU.mult).then_inc(rows_ready, 1)

            layer_norm(1, x_arrived)
            normalise(1, 0, NK)

            dve.wait_ge(spans_turned, 1)
            V.tensor_copy(low, bank[0][0:1, 0:CHUNKS])

            def by_group(v):
                return v.rearrange("a (g c) -> a g c", c=GROUP_CHUNKS)

            def of_first(v):
                return by_group(v)[:, :, 0:1].to_broadcast([1, GROUPS, GROUP_CHUNKS])

            dve.drain()
            V.tensor_tensor(spread, bank[1][0:1, 0:CHUNKS], low, ALU.subtract)
            V.tensor_tensor(by_group(place_in_group), by_group(low), of_first(low), ALU.subtract)
            dve.drain()
            V.tensor_reduce(flag[:, 0:1], spread, AX.X, ALU.max)
            V.tensor_reduce(flag[:, 1:2], place_in_group, AX.X, ALU.max)
            V.tensor_reduce(flag[:, 2:3], place_in_group, AX.X, ALU.min)
            dve.drain()
            V.tensor_scalar(flag[:, 0:1], flag[:, 0:1], float(WIN - 1), None, ALU.is_le)
            V.tensor_scalar(flag[:, 1:2], flag[:, 1:2], float(GROUP_WIN - WIN), None, ALU.is_le)
            V.tensor_scalar(flag[:, 2:3], flag[:, 2:3], 0.0, None, ALU.is_ge)
            dve.drain()
            V.tensor_tensor(flag[:, 3:4], flag[:, 0:1], flag[:, 1:2], ALU.mult)
            dve.drain()
            one_pass = flag[:, 4:5]
            V.tensor_tensor(one_pass, flag[:, 3:4], flag[:, 2:3], ALU.mult)
            dve.drain()
            V.tensor_scalar(first_start, low, one_pass, None, ALU.mult)
            V.tensor_scalar(flag[:, 5:6], one_pass, float(-WIN), float(WIN), ALU.mult, ALU.add)
            V.tensor_scalar(passes_i[:, :], one_pass, float(1 - WINDOW_PASSES), float(WINDOW_PASSES),
                            ALU.mult, ALU.add).then_inc(passes_ready, 1)
            step, moved = flag[:, 5:6], flag[:, 6:7]

            for l in range(2):
                S = L[l]
                res = cols[1 - l]
                dve.sem_inc(S["added"], ADDED_CREDIT)
                dve.sem_inc(S["w_added"], H)
                V.memset(moved, 0.0)

                def windows(k):
                    dve.drain()
                    V.tensor_scalar(start_row[:, :], first_start, moved, None, ALU.add).then_inc(S["starts"], 1)
                    dve.drain()
                    V.tensor_tensor(moved, moved, step, ALU.add)
                    V.tensor_tensor(by_group(off_f), by_group(start_row[:, :]), of_first(start_row[:, :]),
                                    ALU.subtract)
                    V.tensor_copy(base_i[:, :], by_group(start_row[:, :])[:, :, 0])
                    dve.drain()
                    V.tensor_copy(off_i[:, :], off_f)
                    dve.wait_ge(edges_copied, 3)
                    dve.wait_ge(S["starts_wide"], k + 1)
                    V.tensor_tensor(key_t[:, 0, :], edges_t[:, 0, 0:CHUNKS], bank[0][:P, 0:CHUNKS], ALU.subtract)
                    dve.drain()
                    V.tensor_tensor(key_t[:, 1, :], key_t[:, 0, :], edges_t[:, 1, 0:CHUNKS], ALU.add)
                    V.tensor_scalar(key_t[:, 2, :], key_t[:, 0, :], 0.0, None, ALU.is_ge)
                    dve.drain()
                    V.scalar_tensor_tensor(key_t[:, 2, :], key_t[:, 0, :], float(WIN), key_t[:, 2, :],
                                           ALU.is_lt, ALU.mult)
                    dve.drain()
                    V.tensor_tensor(key_t[:, 1, :], key_t[:, 1, :], key_t[:, 2, :], ALU.mult)
                    dve.drain()
                    V.tensor_scalar(key[:, 0:CHUNKS], key_t[:, 1, :], -1.0, None, ALU.add)
                    dve.drain()

                def one_hot(c, u):
                    V.tensor_scalar(hot[:, u % HOTS, :], key_iota[:, :], key[:, bass.ds(c, 1)],
                                    None, ALU.is_equal).then_inc(S["hot"], 1)

                def add_chunk(chunks, buf, off, u):
                    at = accum[:, bass.ds(buf, SPAN)].rearrange("c (h r n) -> c h r n", h=H, r=R)\
                        [:, :, :, bass.ds(off, WIN)]
                    dve.wait_ge(S["summed"], chunks + (u + SUMMED_CREDIT + 1))
                    dve.wait_ge(S["added"], chunks + (u + ADDED_CREDIT))
                    V.tensor_tensor(at, chunk_sum[u % SUMS].rearrange("c h (r n) -> c h r n", r=R), at, ALU.add)\
                        .then_inc(S["added"], 1)

                def add_weighted(k, g, ho):
                    base = dve.value_load(base_i[0:1, bass.ds(g - 1, 1)], min_val=0, max_val=NPAD - GROUP_WIN)
                    at = res[:, ho, bass.ds(base, GROUP_WIN)]
                    dve.wait_ge(S["w_done"], k * (GROUPS * H) + g * H + (ho + 3))
                    dve.wait_ge(S["w_added"], k * (GROUPS * H) + g * H + ho)
                    V.tensor_tensor(at, bank[2 + ho][:, 0:GROUP_WIN], at, ALU.add).then_inc(S["w_added"], 1)

                def group(k, g, first=False):
                    chunks = in_register(dve, k * CHUNKS + g * GROUP_CHUNKS)
                    column = in_register(dve, g * GROUP_CHUNKS)
                    buf = in_register(dve, (g % 2) * SPAN)
                    for u in range(GROUP_CHUNKS):
                        if u % OFFSETS == 0:
                            dve.load(off_regs, off_i[0:1, bass.ds(column + u, OFFSETS)])
                            offs = [dve.snap(r, min_val=0, max_val=GROUP_WIN - WIN) for r in off_regs]
                        if u == 0:
                            dve.wait_ge(S["zeroed"], k * GROUPS + g + 1)
                        add_chunk(chunks, buf, offs[u % OFFSETS], u)
                        one_hot(column + (u + HOTS), u)
                        if l == 1 and isinstance(k, int) and first and u == SUMS:
                            V.tensor_scalar(cols[1][:, 0, 0:N], cols[1][:, 0, 0:N], 0.0, None, ALU.max)\
                                .then_inc(L[0]["relu"], 1)
                        if not first and u in (GROUP_CHUNKS // 2 + 1, GROUP_CHUNKS - 1):
                            add_weighted(k, g, int(u == GROUP_CHUNKS - 1))

                passes = passes_of(dve)

                def one_pass(k):
                    if l == 1 and isinstance(k, int):
                        dve.wait_ge(L[0]["back"], NK // 2)
                    windows(k)
                    for u in range(HOTS):
                        one_hot(u, u)
                    group(k, 0, first=True)
                    if isinstance(k, int):
                        dve.wait_ge(S["self_out"], SELF_BLOCKS * H)
                    with dve.Fori(1, GROUPS) as g:
                        group(k, g)
                    for ho in range(H):
                        add_weighted(k, GROUPS, ho)

                one_pass(0)
                with dve.If(passes > 1):
                    with dve.Fori(1, passes) as k:
                        one_pass(k)
                dve.drain().then_inc(S["complete"], 1)
                if l == 0:
                    for i in range(1, NK // 2, 2):
                        dve.wait_ge(S["back"], i + 1)
                        V.tensor_scalar(f_rows[:, 2 * i:2 * i + 2, :],
                                        bank[4 + i % 4][:P, :].rearrange("p (k d) -> p k d", k=2), 0.0, None, ALU.max)\
                            .then_inc(S["back_v"], 1)
                else:
                    for i in range(NK // 2):
                        dve.wait_ge(S["back"], i + 1)
                        V.tensor_tensor(x_rows[:, 2 * i:2 * i + 2, :], x_rows[:, 2 * i:2 * i + 2, :],
                                        bank[4 + i % 4][:P, :].rearrange("p (k d) -> p k d", k=2), ALU.add)\
                            .then_inc(S["back_v"], 1)

            layer_norm(2, lambda k: dve.wait_ge(L[1]["back_v"], k // 2 + 1))

            def split_w1(e):
                dve.wait_ge(w1_hi, e + 1)
                V.tensor_tensor(w_lo[:, 0:2048], w_raw[:, 0:2048], w_hi[:, 0:2048].bitcast(F32), ALU.subtract)\
                    .then_inc(w1_split, 1)

            wide = [P, NK, EXPERTS]
            parts = [gate_parts[:, i] for i in range(2)]
            dve.wait_ge(norm_gate_out, 1)
            V.tensor_tensor(parts[0], norm_gate[:, 0:NK, :], norms[:, 0, 4, :, None].to_broadcast(wide), ALU.mult)
            V.tensor_tensor(tok[:, 8, :], mean[0], mean[1], ALU.subtract)
            dve.drain()
            V.tensor_tensor(parts[1], norm_gate[:, NK:NK + 1, :].to_broadcast(wide),
                            tok[:, 8, :, None].to_broadcast(wide), ALU.mult)
            dve.drain()
            V.tensor_tensor(parts[0], parts[0], parts[1], ALU.add)
            normalise(2, 0, 5)
            dve.drain()
            dve.wait_ge(gate_in, 2 * 16)
            dve.wait_ge(gate_turned, 2)
            V.tensor_tensor(lg[:, 0], bank[3][:P, 0:NK * EXPERTS].rearrange("p (k e) -> p k e", k=NK), parts[0],
                            ALU.add)
            dve.drain()
            V.tensor_tensor(lg[:, 0], lg[:, 0], inv_std[1][:, :, None].to_broadcast(wide), ALU.mult)
            dve.drain()
            V.tensor_tensor(lg[:, 0], lg[:, 0], gate_b[:, None, :].to_broadcast(wide), ALU.add)
            dve.drain()
            V.tensor_reduce(tok[:, 0, :], lg[:, 0], AX.X, ALU.max)
            dve.drain()
            V.tensor_tensor(lg[:, 0], lg[:, 0], tok[:, 0, :, None].to_broadcast(wide), ALU.subtract)\
                .then_inc(scores_ready, 1)
            normalise(2, 5, 9)
            dve.wait_ge(exps_ready, 1)
            V.tensor_reduce(tok[:, 1, :], lg[:, 1], AX.X, ALU.add)
            dve.drain()
            V.reciprocal(tok[:, 2, :], tok[:, 1, :])
            dve.drain()
            V.tensor_tensor(lg[:, 2], lg[:, 1], tok[:, 2, :, None].to_broadcast(wide), ALU.mult)
            dve.drain()
            best = tok[:, 3, :]
            V.tensor_reduce(best, lg[:, 2], AX.X, ALU.max)
            dve.drain()
            V.tensor_tensor(lg[:, 3], lg[:, 2], tok[:, 3, :, None].to_broadcast(wide), ALU.is_equal)
            dve.drain()
            V.scalar_tensor_tensor(lg[:, 0], e_iota[:, None, :].to_broadcast(wide), float(-EXPERTS), lg[:, 3],
                                   ALU.add, ALU.mult)
            dve.drain()
            V.tensor_reduce(tok[:, 4, :], lg[:, 0], AX.X, ALU.min)
            dve.drain()
            V.tensor_scalar(tok[:, 5, :], tok[:, 4, :], 0.0, float(-EXPERTS), ALU.is_equal, ALU.mult)
            dve.drain()
            V.tensor_tensor(tok[:, 4, :], tok[:, 4, :], tok[:, 5, :], ALU.add)
            dve.drain()
            for e in range(EXPERTS):
                V.tensor_scalar(picked[:, e, :], tok[:, 4, :], float(e - EXPERTS), None, ALU.is_equal)
            dve.drain()
            for e in range(EXPERTS):
                last = V.tensor_tensor_scan(counts[:, e, :], picked[:, e, :], zeros[:P, 0:NK], 0.0, ALU.add, ALU.add)
            last.then_inc(totals_ready, 1)
            normalise(2, 9, 13)
            dve.wait_ge(before_ready, 1)
            place = lg[:, 1].rearrange("p k e -> p (k e)").rearrange("p (e k) -> p e k", e=EXPERTS)
            V.tensor_tensor(place, counts[:, :, :],
                            bank[3][:P, 0:EXPERTS, None].to_broadcast([P, EXPERTS, NK]), ALU.add)
            dve.drain()
            V.tensor_tensor(place, place, picked[:, :, :], ALU.mult)
            dve.drain()
            V.tensor_reduce(tok[:, 5, :], place.rearrange("p e k -> p k e"), AX.X, ALU.add)
            dve.drain()
            kept = tok[:, 6, :]
            V.tensor_scalar(kept, tok[:, 5, :], float(CAP), None, ALU.is_le)
            V.scalar_tensor_tensor(tok[:, 7, :], tok[:, 4, :], float(SLOTS), tok[:, 5, :], ALU.mult, ALU.add)
            dve.drain()
            V.tensor_scalar(tok[:, 7, :], tok[:, 7, :], float(EXPERTS * SLOTS - 1), None, ALU.add)
            V.tensor_scalar(tok[:, 9, :], kept, float(-NO_ROW), float(NO_ROW), ALU.mult, ALU.add)
            V.tensor_scalar(tok[:, 10, :], kept, float(NO_ROW), None, ALU.mult)
            dve.drain()
            V.tensor_tensor(tok[:, 9, :], tok[:, 7, :], tok[:, 9, :], ALU.add)
            dve.drain()
            V.tensor_copy(slot_to[:, :], tok[:, 9, :])
            V.tensor_tensor(tok[:, 10, :], tok[:, 10, :], token_f[:, :], ALU.add)
            V.tensor_copy(token_info[:, :, 0], token_f[:, :])
            V.tensor_copy(token_info[:, :, 1].bitcast(F32), best)
            dve.drain()
            V.tensor_copy(token_over[:, :], tok[:, 10, :])
            dve.drain().then_inc(slots_ready, 1)
            normalise(2, 13, NK)

            def result(half, v, tiles=slice(0, SLOT_TILES)):
                e = half * 2 + v
                dve.wait_ge(y_scaled, e * SLOT_TILES + tiles.stop)
                V.tensor_scalar(y_finite[:, tiles, :], y_raw[v][:, tiles, :], 0.0, 0.0, ALU.mult, ALU.is_equal)
                V.tensor_scalar(y_over[:, tiles, :], y_raw[v][:, tiles, :], FLT_MAX, NAN_INF_TO, ALU.is_gt, ALU.mult)
                V.tensor_scalar(y_under[:, tiles, :], y_raw[v][:, tiles, :], -FLT_MAX, -NAN_INF_TO, ALU.is_lt, ALU.mult)
                dve.drain()
                if not (isinstance(half, int) and half == 0):
                    dve.wait_ge(y_sent[v], half * (SLOT_TILES * 16))
                V.tensor_tensor(y_out[v][:, tiles, :], y_over[:, tiles, :], y_under[:, tiles, :], ALU.add)
                dve.drain()
                V.copy_predicated(y_out[v][:, tiles, :], y_finite[:, tiles, :], y_raw[v][:, tiles, :])
                dve.drain()
                dve.wait_ge(slot_res_in[v], half * 16 + 16)
                V.tensor_tensor(y_out[v][:, tiles, :], y_out[v][:, tiles, :], slot_res[v][:, tiles, :], ALU.add)\
                    .then_inc(y_result, 1)

            def split_slots(e):
                for h in range(H):
                    dve.wait_ge(slots_hi, e * H + (h + 1))
                    V.tensor_tensor(slot_lo[:, h, :], bank[4 + h][:, 0:SLOTS], slot_hi[:, h, :].bitcast(F32),
                                    ALU.subtract).then_inc(slots_split, 1)

            def expert(half, v, first=False, last=False):
                e = half * 2 + v
                for q in range(FT // 2):
                    two = slice(2 * q, 2 * q + 2)
                    dve.wait_ge(mid_out, e * FT + (2 * q + 2))
                    V.tensor_copy(mid_hi[:, two, :], mid_full[:, two, :])
                    dve.drain()
                    V.tensor_tensor(mid_lo[:, two, :], mid_full[:, two, :], mid_hi[:, two, :].bitcast(F32),
                                    ALU.subtract).then_inc(mid_split, 1)
                    at = 2048 + q * 512
                    dve.wait_ge(w2_hi, e * 4 + (q + 1))
                    V.tensor_tensor(w_lo[:, at:at + 512], w_raw[:, at:at + 512], w_hi[:, at:at + 512].bitcast(F32),
                                    ALU.subtract).then_inc(w2_split, 1)
                if not last:
                    split_w1(e + 1)
                    split_slots(e + 1)
                if not first:
                    result(half - (1 - v), 1 - v)

            split_w1(0)
            split_slots(0)
            expert(0, 0, first=True)
            expert(0, 1)
            with dve.Fori(1, EXPERTS // 2 - 1) as half:
                for v in range(2):
                    expert(half, v)
            expert(EXPERTS // 2 - 1, 0)
            expert(EXPERTS // 2 - 1, 1, last=True)
            for j in range(0, SLOT_TILES, 2):
                result(EXPERTS // 2 - 1, 1, slice(j, j + 2))


INPUTS = ["x", "src", "dst", "edge_type_8", "L0_gnn_W1", "L0_gnn_self_w1", "L0_gnn_b1", "L0_gnn_W2",
          "L0_gnn_self_w2", "L0_gnn_b2", "L0_ffn_gate_w", "L0_ffn_gate_b", "L0_ffn_w1", "L0_ffn_b1",
          "L0_ffn_w2", "L0_ffn_b2"]


SHAPES = {"x": (N, D), "src": (E,), "dst": (E,), "edge_type_8": (E,),
          "L0_ffn_gate_w": (D, EXPERTS), "L0_ffn_gate_b": (EXPERTS,), "L0_ffn_w1": (EXPERTS, D, FF),
          "L0_ffn_b1": (EXPERTS, FF), "L0_ffn_w2": (EXPERTS, FF, D), "L0_ffn_b2": (EXPERTS, D)}
for _l in "12":
    SHAPES |= {f"L0_gnn_W{_l}": (R, D, D), f"L0_gnn_self_w{_l}": (D, D), f"L0_gnn_b{_l}": (D,)}


def declare(nc):
    io = {n: nc.dram_tensor(f"in_{n}", SHAPES[n], I32 if n in ("src", "dst", "edge_type_8") else F32,
                            kind="ExternalInput").ap() for n in INPUTS}
    build(nc, io, nc.dram_tensor("out", (N, D), F32, kind="ExternalOutput").ap())


def kernel(**inputs):
    import concourse.bacc as bacc
    from concourse.bass_utils import run_bass_kernel_spmd

    nc = bacc.Bacc("TRN2", target_bir_lowering=False, num_devices=1)
    declare(nc)
    arrays = {f"in_{n}": np.ascontiguousarray(inputs[n]) for n in INPUTS}
    return run_bass_kernel_spmd(nc, [arrays], core_ids=[0]).results[0]["out"]
```
